# Optimizing a Trainium2 kernel written in Bass

```python
import numpy as np
import jax
import jax.numpy as jnp

def _softmax(x, axis=-1):
    return jax.nn.softmax(x, axis=axis)

def _gelu(x):
    return jax.nn.gelu(x, approximate=True)

def _silu(x):
    return jax.nn.silu(x)

def _sigmoid(x):
    return jax.nn.sigmoid(x)

def _layernorm(x, axis=-1, eps=1e-05):
    m = jnp.mean(x, axis=axis, keepdims=True)
    v = jnp.var(x, axis=axis, keepdims=True)
    return (x - m) / jnp.sqrt(v + eps)

def _scatter_add(tgt, idx, src, axis=0):
    return tgt.at[idx].add(src)

def _segment_sum(src, seg, n):
    return jax.ops.segment_sum(src, seg, n)
kernel_name = 'mk_dlrm_tower_d1_rec_r8_030a97'

def setup_inputs(seed: int=0):
    np.random.seed(seed)
    _w = jnp.asarray

    def _rec_inputs():
        import jax
        import jax.numpy as jnp
        _tk = jax.random.key(seed)
        dense_ctx = jax.random.normal(jax.random.fold_in(_tk, 190), (2048, 16), jnp.float32)
        ids = jnp.stack([jax.random.randint(jax.random.fold_in(_tk, 200 + f), (2048,), 0, v, jnp.int32) for f, v in enumerate([12500, 1250, 12500, 125000, 1000, 1250, 12500, 1250, 125000, 1000, 1000, 12500, 1250, 12500, 1000, 1250, 1000, 125000, 12500, 12500, 12500, 1250, 12500, 1000, 1250, 1250, 1250, 1000, 12500, 12500, 12500, 12500, 1000, 1000, 12500, 1000, 12500, 1250, 1000, 1000])], axis=1)
        tbl_0 = 0.05 * jax.random.normal(jax.random.fold_in(_tk, 500 + 0), (12500, 32), jnp.float32)
        tbl_1 = 0.05 * jax.random.normal(jax.random.fold_in(_tk, 500 + 1), (1250, 32), jnp.float32)
        tbl_2 = 0.05 * jax.random.normal(jax.random.fold_in(_tk, 500 + 2), (12500, 32), jnp.float32)
        tbl_3 = 0.05 * jax.random.normal(jax.random.fold_in(_tk, 500 + 3), (125000, 32), jnp.float32)
        tbl_4 = 0.05 * jax.random.normal(jax.random.fold_in(_tk, 500 + 4), (1000, 32), jnp.float32)
        tbl_5 = 0.05 * jax.random.normal(jax.random.fold_in(_tk, 500 + 5), (1250, 32), jnp.float32)
        tbl_6 = 0.05 * jax.random.normal(jax.random.fold_in(_tk, 500 + 6), (12500, 32), jnp.float32)
        tbl_7 = 0.05 * jax.random.normal(jax.random.fold_in(_tk, 500 + 7), (1250, 32), jnp.float32)
        tbl_8 = 0.05 * jax.random.normal(jax.random.fold_in(_tk, 500 + 8), (125000, 32), jnp.float32)
        tbl_9 = 0.05 * jax.random.normal(jax.random.fold_in(_tk, 500 + 9), (1000, 32), jnp.float32)
        tbl_10 = 0.05 * jax.random.normal(jax.random.fold_in(_tk, 500 + 10), (1000, 32), jnp.float32)
        tbl_11 = 0.05 * jax.random.normal(jax.random.fold_in(_tk, 500 + 11), (12500, 32), jnp.float32)
        tbl_12 = 0.05 * jax.random.normal(jax.random.fold_in(_tk, 500 + 12), (1250, 32), jnp.float32)
        tbl_13 = 0.05 * jax.random.normal(jax.random.fold_in(_tk, 500 + 13), (12500, 32), jnp.float32)
        tbl_14 = 0.05 * jax.random.normal(jax.random.fold_in(_tk, 500 + 14), (1000, 32), jnp.float32)
        tbl_15 = 0.05 * jax.random.normal(jax.random.fold_in(_tk, 500 + 15), (1250, 32), jnp.float32)
        tbl_16 = 0.05 * jax.random.normal(jax.random.fold_in(_tk, 500 + 16), (1000, 32), jnp.float32)
        tbl_17 = 0.05 * jax.random.normal(jax.random.fold_in(_tk, 500 + 17), (125000, 32), jnp.float32)
        tbl_18 = 0.05 * jax.random.normal(jax.random.fold_in(_tk, 500 + 18), (12500, 32), jnp.float32)
        tbl_19 = 0.05 * jax.random.normal(jax.random.fold_in(_tk, 500 + 19), (12500, 32), jnp.float32)
        tbl_20 = 0.05 * jax.random.normal(jax.random.fold_in(_tk, 500 + 20), (12500, 32), jnp.float32)
        tbl_21 = 0.05 * jax.random.normal(jax.random.fold_in(_tk, 500 + 21), (1250, 32), jnp.float32)
        tbl_22 = 0.05 * jax.random.normal(jax.random.fold_in(_tk, 500 + 22), (12500, 32), jnp.float32)
        tbl_23 = 0.05 * jax.random.normal(jax.random.fold_in(_tk, 500 + 23), (1000, 32), jnp.float32)
        tbl_24 = 0.05 * jax.random.normal(jax.random.fold_in(_tk, 500 + 24), (1250, 32), jnp.float32)
        tbl_25 = 0.05 * jax.random.normal(jax.random.fold_in(_tk, 500 + 25), (1250, 32), jnp.float32)
        tbl_26 = 0.05 * jax.random.normal(jax.random.fold_in(_tk, 500 + 26), (1250, 32), jnp.float32)
        tbl_27 = 0.05 * jax.random.normal(jax.random.fold_in(_tk, 500 + 27), (1000, 32), jnp.float32)
        tbl_28 = 0.05 * jax.random.normal(jax.random.fold_in(_tk, 500 + 28), (12500, 32), jnp.float32)
        tbl_29 = 0.05 * jax.random.normal(jax.random.fold_in(_tk, 500 + 29), (12500, 32), jnp.float32)
        tbl_30 = 0.05 * jax.random.normal(jax.random.fold_in(_tk, 500 + 30), (12500, 32), jnp.float32)
        tbl_31 = 0.05 * jax.random.normal(jax.random.fold_in(_tk, 500 + 31), (12500, 32), jnp.float32)
        tbl_32 = 0.05 * jax.random.normal(jax.random.fold_in(_tk, 500 + 32), (1000, 32), jnp.float32)
        tbl_33 = 0.05 * jax.random.normal(jax.random.fold_in(_tk, 500 + 33), (1000, 32), jnp.float32)
        tbl_34 = 0.05 * jax.random.normal(jax.random.fold_in(_tk, 500 + 34), (12500, 32), jnp.float32)
        tbl_35 = 0.05 * jax.random.normal(jax.random.fold_in(_tk, 500 + 35), (1000, 32), jnp.float32)
        tbl_36 = 0.05 * jax.random.normal(jax.random.fold_in(_tk, 500 + 36), (12500, 32), jnp.float32)
        tbl_37 = 0.05 * jax.random.normal(jax.random.fold_in(_tk, 500 + 37), (1250, 32), jnp.float32)
        tbl_38 = 0.05 * jax.random.normal(jax.random.fold_in(_tk, 500 + 38), (1000, 32), jnp.float32)
        tbl_39 = 0.05 * jax.random.normal(jax.random.fold_in(_tk, 500 + 39), (1000, 32), jnp.float32)
        _rk = jax.random.fold_in(_tk, 7)
        W_top1 = 0.0354441 * jax.random.normal(jax.random.fold_in(_tk, 801), (796, 512), jnp.float32)
        W_top2 = 0.0441942 * jax.random.normal(jax.random.fold_in(_tk, 802), (512, 256), jnp.float32)
        W_top3 = 0.0625 * jax.random.normal(jax.random.fold_in(_tk, 803), (256, 1), jnp.float32)
        b_top1 = jnp.zeros((512,), jnp.float32)
        b_top2 = jnp.zeros((256,), jnp.float32)
        return (dense_ctx, ids, tbl_0, tbl_1, tbl_2, tbl_3, tbl_4, tbl_5, tbl_6, tbl_7, tbl_8, tbl_9, tbl_10, tbl_11, tbl_12, tbl_13, tbl_14, tbl_15, tbl_16, tbl_17, tbl_18, tbl_19, tbl_20, tbl_21, tbl_22, tbl_23, tbl_24, tbl_25, tbl_26, tbl_27, tbl_28, tbl_29, tbl_30, tbl_31, tbl_32, tbl_33, tbl_34, tbl_35, tbl_36, tbl_37, tbl_38, tbl_39, W_top1, b_top1, W_top2, b_top2, W_top3)
    dense_ctx, ids, tbl_0, tbl_1, tbl_2, tbl_3, tbl_4, tbl_5, tbl_6, tbl_7, tbl_8, tbl_9, tbl_10, tbl_11, tbl_12, tbl_13, tbl_14, tbl_15, tbl_16, tbl_17, tbl_18, tbl_19, tbl_20, tbl_21, tbl_22, tbl_23, tbl_24, tbl_25, tbl_26, tbl_27, tbl_28, tbl_29, tbl_30, tbl_31, tbl_32, tbl_33, tbl_34, tbl_35, tbl_36, tbl_37, tbl_38, tbl_39, W_top1, b_top1, W_top2, b_top2, W_top3 = _rec_inputs()

    def _L0_rec_setup():
        import jax, jax.numpy as jnp
        import numpy as np
        NUM_FIELDS = 40
        EMBED_DIM = 32
        BATCH = 512
        NUM_PAIRS = NUM_FIELDS * (NUM_FIELDS - 1) // 2
        key = jax.random.key(seed)
        k1, k2 = jax.random.split(key)
        inputs = jax.random.normal(k1, (BATCH, NUM_FIELDS, EMBED_DIM), dtype=jnp.float32)
        std = (2.0 / (EMBED_DIM + EMBED_DIM)) ** 0.5
        bilinear_matrices = jax.random.normal(k2, (NUM_PAIRS, EMBED_DIM, EMBED_DIM), dtype=jnp.float32) * std
        return {'inputs': inputs, 'bilinear_matrices': bilinear_matrices}
    _L0_rec_all = _L0_rec_setup()
    _L0_rec_in = {k: v for k, v in _L0_rec_all.items() if k in ('bilinear_matrices',)}
    del _L0_rec_all
    return {'dense_ctx': dense_ctx, 'ids': ids, 'tbl_0': tbl_0, 'tbl_1': tbl_1, 'tbl_2': tbl_2, 'tbl_3': tbl_3, 'tbl_4': tbl_4, 'tbl_5': tbl_5, 'tbl_6': tbl_6, 'tbl_7': tbl_7, 'tbl_8': tbl_8, 'tbl_9': tbl_9, 'tbl_10': tbl_10, 'tbl_11': tbl_11, 'tbl_12': tbl_12, 'tbl_13': tbl_13, 'tbl_14': tbl_14, 'tbl_15': tbl_15, 'tbl_16': tbl_16, 'tbl_17': tbl_17, 'tbl_18': tbl_18, 'tbl_19': tbl_19, 'tbl_20': tbl_20, 'tbl_21': tbl_21, 'tbl_22': tbl_22, 'tbl_23': tbl_23, 'tbl_24': tbl_24, 'tbl_25': tbl_25, 'tbl_26': tbl_26, 'tbl_27': tbl_27, 'tbl_28': tbl_28, 'tbl_29': tbl_29, 'tbl_30': tbl_30, 'tbl_31': tbl_31, 'tbl_32': tbl_32, 'tbl_33': tbl_33, 'tbl_34': tbl_34, 'tbl_35': tbl_35, 'tbl_36': tbl_36, 'tbl_37': tbl_37, 'tbl_38': tbl_38, 'tbl_39': tbl_39, 'W_top1': W_top1, 'b_top1': b_top1, 'W_top2': W_top2, 'b_top2': b_top2, 'W_top3': W_top3, 'L0_rec_bilinear_matrices': _L0_rec_in['bilinear_matrices']}

def reference(dense_ctx, ids, tbl_0, tbl_1, tbl_2, tbl_3, tbl_4, tbl_5, tbl_6, tbl_7, tbl_8, tbl_9, tbl_10, tbl_11, tbl_12, tbl_13, tbl_14, tbl_15, tbl_16, tbl_17, tbl_18, tbl_19, tbl_20, tbl_21, tbl_22, tbl_23, tbl_24, tbl_25, tbl_26, tbl_27, tbl_28, tbl_29, tbl_30, tbl_31, tbl_32, tbl_33, tbl_34, tbl_35, tbl_36, tbl_37, tbl_38, tbl_39, W_top1, b_top1, W_top2, b_top2, W_top3, L0_rec_bilinear_matrices):
    import jax
    import jax.numpy as jnp

    def _L0_rec_ref(inputs, bilinear_matrices):
        import jax, jax.numpy as jnp
        import numpy as np
        NUM_FIELDS = 40
        EMBED_DIM = 32
        BATCH = 512
        NUM_PAIRS = NUM_FIELDS * (NUM_FIELDS - 1) // 2
        num_fields = inputs.shape[1]
        iidx, jidx = jnp.triu_indices(num_fields, k=1)
        xi = inputs[:, iidx, :]
        xj = inputs[:, jidx, :]
        out = jnp.einsum('bpd,pde,bpe->bp', xi, bilinear_matrices, xj)
        return out
    e = jnp.stack([tbl_0[ids[:, 0]], tbl_1[ids[:, 1]], tbl_2[ids[:, 2]], tbl_3[ids[:, 3]], tbl_4[ids[:, 4]], tbl_5[ids[:, 5]], tbl_6[ids[:, 6]], tbl_7[ids[:, 7]], tbl_8[ids[:, 8]], tbl_9[ids[:, 9]], tbl_10[ids[:, 10]], tbl_11[ids[:, 11]], tbl_12[ids[:, 12]], tbl_13[ids[:, 13]], tbl_14[ids[:, 14]], tbl_15[ids[:, 15]], tbl_16[ids[:, 16]], tbl_17[ids[:, 17]], tbl_18[ids[:, 18]], tbl_19[ids[:, 19]], tbl_20[ids[:, 20]], tbl_21[ids[:, 21]], tbl_22[ids[:, 22]], tbl_23[ids[:, 23]], tbl_24[ids[:, 24]], tbl_25[ids[:, 25]], tbl_26[ids[:, 26]], tbl_27[ids[:, 27]], tbl_28[ids[:, 28]], tbl_29[ids[:, 29]], tbl_30[ids[:, 30]], tbl_31[ids[:, 31]], tbl_32[ids[:, 32]], tbl_33[ids[:, 33]], tbl_34[ids[:, 34]], tbl_35[ids[:, 35]], tbl_36[ids[:, 36]], tbl_37[ids[:, 37]], tbl_38[ids[:, 38]], tbl_39[ids[:, 39]]], axis=1)
    z = _L0_rec_ref(e, L0_rec_bilinear_matrices)
    z = z.reshape(z.shape[0], -1)
    h = jnp.concatenate([z, dense_ctx], axis=1)
    h = jnp.maximum(h @ W_top1 + b_top1, 0.0)
    h = jnp.maximum(h @ W_top2 + b_top2, 0.0)
    y = h @ W_top3
    return y

_drawn_inputs = setup_inputs


def setup_inputs(seed=0):
    import zlib

    import numpy as np

    out = dict(_drawn_inputs(seed))
    spreads = {'b_top1': (0.0, 0.1), 'b_top2': (0.0, 0.1)}
    factors = {'tbl_0': 3.624,
     'tbl_1': 3.221,
     'tbl_2': 3.435,
     'tbl_3': 3.064,
     'tbl_4': 3.268,
     'tbl_5': 2.983,
     'tbl_6': 3.446,
     'tbl_7': 3.308,
     'tbl_8': 3.029,
     'tbl_9': 3.044,
     'tbl_10': 3.176,
     'tbl_11': 3.597,
     'tbl_12': 2.944,
     'tbl_13': 3.156,
     'tbl_14': 3.229,
     'tbl_15': 3.376,
     'tbl_16': 3.348,
     'tbl_17': 3.166,
     'tbl_18': 3.578,
     'tbl_19': 3.34,
     'tbl_20': 2.996,
     'tbl_21': 3.405,
     'tbl_22': 3.254,
     'tbl_23': 3.08,
     'tbl_24': 3.379,
     'tbl_25': 3.344,
     'tbl_26': 3.083,
     'tbl_27': 3.47,
     'tbl_28': 3.199,
     'tbl_29': 3.242,
     'tbl_30': 3.38,
     'tbl_31': 3.018,
     'tbl_32': 3.316,
     'tbl_33': 3.337,
     'tbl_34': 3.269,
     'tbl_35': 3.178,
     'tbl_36': 3.533,
     'tbl_37': 3.39,
     'tbl_38': 3.503,
     'tbl_39': 3.204}
    for name, (base, spread) in spreads.items():
        noise = np.random.default_rng([zlib.crc32(name.encode()), seed]).standard_normal(out[name].shape)
        drawn = base * np.exp(spread * noise) if base else spread * noise
        out[name] = jnp.asarray(drawn.astype(out[name].dtype))
    for name, factor in factors.items():
        out[name] = (out[name] * factor).astype(out[name].dtype)
    return out
```

```python
from contextlib import ExitStack

import numpy as np

import concourse.bass as bass
from concourse import mybir

F32 = mybir.dt.float32
F32R = mybir.dt.float32r
I32 = mybir.dt.int32
ALU = mybir.AluOpType
ACT = mybir.ActivationFunctionType
AX = mybir.AxisListType

NF = 40
E = 32
B = 2048
P = 128
TILES = B // P
NPAIR = NF * (NF - 1) // 2
DENSE = 16
H1, H2 = 512, 256
DIN = NPAIR + DENSE
BANK = 512
RUN = BANK // E
GF = 4
NG = NF // GF
LF = 8
NL = NF // LF
KC = (DIN + P - 1) // P
KLAST = DIN - (KC - 1) * P
M1, M2 = H1 // P, H2 // P
DRING = 3
SRING = 4


class Region:

    def __init__(self, kind, b, j0=0, nj=0, diag=None):
        self.kind, self.b, self.j0, self.nj, self.diag = kind, b, j0, nj, diag
        self.ii = [2 * x for x in diag] if diag else [2 * b, 2 * b + 1]
        self.n = len(diag) if diag else 2 * nj
        self.js = [2 * x + 1 for x in diag] if diag else list(range(j0, j0 + nj))
        self.z = None
        self.block = None

    def pairs(self):
        if self.diag:
            return [(i, i + 1) for i in self.ii]
        return [(i, j) for i in self.ii for j in self.js]


def chunks(kind, b):
    total = NF - 2 - 2 * b
    k = -(-total // RUN)
    out, j = [], 2 * b + 2
    for c in range(k):
        nj = total // k + (c < total % k)
        out.append(Region(kind, b, j, nj))
        j += nj
    return out


class Plan:

    PROWS = 6
    BLOCKS = (4, 5, 3, 3)

    def __init__(self):
        p_regions = []
        for b in range(self.PROWS):
            p_regions += chunks("P", b)
        assert sum(self.BLOCKS) == len(p_regions)
        for k, r in zip([k for k, m in enumerate(self.BLOCKS) for _ in range(m)], p_regions):
            r.block = k
        nb = NF // 2
        d_regions = []
        for b in range(self.PROWS, nb - 1):
            d_regions += chunks("D", b)
        d_regions.insert(13, Region("D", None, diag=list(range(0, 6))))
        d_regions.insert(17, Region("D", None, diag=list(range(6, 13))))
        d_regions.append(Region("D", None, diag=list(range(13, 20))))
        steps, ip, idd = [], 0, 0
        while ip < len(p_regions) or idd < len(d_regions):
            if idd * len(p_regions) <= ip * len(d_regions) and idd < len(d_regions) or ip == len(p_regions):
                steps.append(d_regions[idd])
                idd += 1
            else:
                steps.append(p_regions[ip])
                ip += 1
        self.steps = steps
        self.ns = len(steps)
        self.nd = len(d_regions)
        self.nblk = len(self.BLOCKS)
        z = 0
        self.blk_z, self.blk_n, self.blk_first, self.blk_last = [], [], [], []
        for k in range(self.nblk):
            rs = [r for r in p_regions if r.block == k]
            self.blk_z.append(z)
            for r in rs:
                r.z = z
                z += r.n
            self.blk_n.append(z - self.blk_z[-1])
            self.blk_first.append(min(steps.index(r) for r in rs))
            self.blk_last.append(max(steps.index(r) for r in rs))
        for r in steps:
            if r.kind == "D":
                r.z = z
                z += r.n
        assert z == NPAIR
        self.pairs = [None] * NPAIR
        for r in steps:
            for k, pr in enumerate(r.pairs()):
                self.pairs[r.z + k] = pr
        assert sorted(self.pairs) == [(i, j) for i in range(NF) for j in range(i + 1, NF)]
        self.d_index = {s: k for k, s in enumerate(s for s, r in enumerate(steps) if r.kind == "D")}
        assert self.ns % 2 == 0 and self.nblk % 2 == 0 and self.nd % DRING == 0
        first = [min(s for s, r in enumerate(steps) if any(i // GF == g for i in r.ii)) for g in range(NG)]
        last = [max(s for s, r in enumerate(steps) if any(i // GF == g for i in r.ii)) for g in range(NG)]
        self.group_order = sorted(range(NG), key=lambda g: first[g])
        at, nxt = {}, 10 ** 9
        for g in reversed(self.group_order):
            at[g] = min(first[g] - self.LEAD, nxt - 2)
            nxt = at[g]
        self.tr_at, self.hi_at, self.lo_at, self.dup_at = {}, {}, {}, {}
        for q, g in enumerate(self.group_order):
            a = at[g]
            assert a + self.ns > last[g], (g, a, last[g])
            self.put(self.tr_at, a, (q, g))
            self.put(self.hi_at, a - 5, (q, g))
            self.put(self.lo_at, a - 4, (q, g))
            self.put(self.dup_at, a - 2, (q, g))
        self.sum_at = {}
        for k in range(self.nblk):
            a = self.blk_last[k] + 2
            b = (self.blk_last[k + 1] if k + 1 < self.nblk else self.ns + self.blk_last[0]) + 2
            n = b - a
            for x in range(n):
                lo, hi = E * x // n, E * (x + 1) // n
                if hi > lo:
                    self.put(self.sum_at, a + x, (k, lo, hi))
        self.sum_end = {k: s for s, v in self.sum_at.items() for (k, lo, hi), _ in v if hi == E}
        a = self.blk_last[0] + 4
        self.mlp_at = {a: [("zt", 0)], a + 2: [("zt", 1)]}
        for m in range(M1):
            self.mlp_at[a + 4 + 2 * m] = [("h1", (m, 0, 4))]
            self.mlp_at[a + 5 + 2 * m] = [("h1", (m, 4, KC))]
        self.mlp_at[a + 4 + 2 * M1 + 1] = [("h2", 0)]
        self.mlp_at[a + 4 + 2 * M1 + 2] = [("h2", 1)]
        self.mlp_at[a + 4 + 2 * M1 + 4] = [("y", 0)]
        assert max(self.mlp_at) < self.ns
        self.load_first = {}
        for k in range(NL):
            s = min(s for s, r in enumerate(steps) if any(j // LF == k for j in r.js))
            self.load_first.setdefault(s, []).append(k)
        self.load_last = []
        for k in range(NL):
            s = max(s for s, r in enumerate(steps) if any(j // LF == k for j in r.js))
            t = max(x + 1 for x, v in self.lo_at.items() for (q, g), dt in v
                    for x in [x - dt * self.ns] if g * GF // LF == k)
            self.load_last.append(max(s, t))
        assert max(self.load_last) < self.ns

    LEAD = 4

    def put(self, table, s, what):
        dt = -(s // self.ns)
        table.setdefault(s % self.ns, []).append((what, dt))


def build_tower(nc, args, out):
    plan = Plan()
    steps, ns, nd, nblk = plan.steps, plan.ns, plan.nd, plan.nblk
    nbmax = [max(plan.blk_n[k::2]) for k in range(2)]
    ndmax = max(r.n for r in steps if r.kind == "D")
    tables = [args[f"tbl_{f}"] for f in range(NF)]
    ids, dense = args["ids"], args["dense_ctx"]
    out_rows = out.rearrange("(t b) o -> t (o b)", b=P)

    with ExitStack() as ctx:
        def sb(name, shape, dt=F32):
            return ctx.enter_context(nc.sbuf_tensor(name, shape, dt))

        def psum(name, shape, dt=F32):
            return ctx.enter_context(nc.psum_tensor(name, shape, dt))

        def sem(name):
            return ctx.enter_context(nc.semaphore(name))

        w_stack = sb("w_stack", [P, NPAIR * E], F32R)
        x_stack = sb("x_stack", [P, NF * P], F32R)
        prod_blk = [sb(f"prod_blk{k}", [P, E, nbmax[k]]) for k in range(2)]
        prod_d = sb("prod_d", [P, DRING, ndmax * E])
        emb = [sb(f"emb{k}", [P, NF * E]) for k in range(2)]
        split = sb("split", [P, SRING, GF, 2, 2, E])
        idx = [sb(f"idx{k}", [P, NF], I32) for k in range(2)]
        z = [sb(f"z{k}", [P, DIN]) for k in range(2)]
        zt = sb("zt", [P, KC, P])
        h1t = sb("h1t", [P, M1, P])
        h2t = sb("h2t", [P, M2, P])
        y_row = sb("y_row", [1, P])
        w1 = sb("w1", [P, KC, H1])
        w2 = sb("w2", [P, M1, H2])
        w3 = sb("w3", [P, M2])
        b1 = sb("b1", [P, M1])
        b2 = sb("b2", [P, M2])
        ident = sb("ident", [P, P])

        t_ps = psum("t_ps", [P, 2, 2 * BANK])
        stack_ps = psum("stack_ps", [P, GF * P])
        sum_ps = psum("sum_ps", [P, BANK])
        zt_ps = psum("zt_ps", [P, BANK])
        h_ps = psum("h_ps", [P, BANK])

        w_staged = [sem(f"w_staged{k}") for k in range(2)]
        w_rounded = sem("w_rounded")
        w_split = sem("w_split")
        consts_in = sem("consts_in")
        idx_in = [sem(f"idx_in{k}") for k in range(2)]
        dense_in = [sem(f"dense_in{k}") for k in range(2)]
        gathered = [[sem(f"gathered{k}_{g}") for g in range(NL)] for k in range(2)]
        gather_may_start = sem("gather_may_start")
        hi_done = sem("hi_done")
        lo_done = sem("lo_done")
        dup_done = sem("dup_done")
        stack_tr = sem("stack_tr")
        stack_ready = sem("stack_ready")
        t_ready = sem("t_ready")
        prod_done = sem("prod_done")
        dsum_done = sem("dsum_done")
        bsum_done = sem("bsum_done")
        bsum_saved = sem("bsum_saved")
        zt_done = sem("zt_done")
        zt_saved = sem("zt_saved")
        h1_done = sem("h1_done")
        h1_saved = sem("h1_saved")
        h2_done = sem("h2_done")
        h2_saved = sem("h2_saved")
        y_done = sem("y_done")
        y_saved = sem("y_saved")
        y_stored = sem("y_stored")

        WCH = 8
        wcols = NPAIR * E // WCH
        assert wcols <= E * min(nbmax) and wcols * WCH == NPAIR * E
        stage = [b[:].rearrange("p e n -> p (e n)")[:, 0:wcols] for b in prod_blk]

        def emb_pairs(r, buf):
            if r.diag:
                a = emb[buf][:, :].rearrange("p (b two e) -> p b two e", two=2, e=E)
                return a[:, r.diag[0]:r.diag[-1] + 1, 1, :]
            a = emb[buf][:, r.j0 * E:(r.j0 + r.nj) * E].rearrange("p (o n e) -> p o n e", o=1, e=E)
            return a.to_broadcast([P, 2, r.nj, E])

        def t_pairs(r, s):
            if r.diag:
                return t_ps[:, s % 2, 0:r.n * E].rearrange("p (n e) -> p n e", e=E)
            a = t_ps[:, s % 2, :].rearrange("p (two n e) -> p two n e", two=2, e=E)
            return a[:, :, 0:r.nj, :]

        def q_slot(par, q):
            return ((par % 2) * NG + q) % SRING

        assert 2 * NG % SRING == 0

        def walk(engine, step):
            last = TILES // 2 - 1
            for s in range(ns):
                step(s, -1, 1, False, False, True)
            for par in range(2):
                for s in range(ns):
                    step(s, 0, par, par > 0, True, True)
            with engine.Fori(1, last) as n:
                for par in range(2):
                    for s in range(ns):
                        step(s, n, par, True, True, True)
            for par in range(2):
                for s in range(ns):
                    step(s, last, par, True, True, par == 0)
            for s in range(ns):
                step(s, last + 1, 0, True, False, False)

        block = ctx.enter_context(nc.Block())

        @block.sync
        def _(sp):
            def load_rows(n, par):
                t = 2 * n + par
                for g in range(NL):
                    if not (isinstance(n, int) and n == 0):
                        sp.wait_ge(gathered[par][g], n * (LF * 16))
                sp.dma_start(idx[par][:, :], ids[bass.ds(t * P, P), :]).then_inc(idx_in[par], 16)
                if not (isinstance(n, int) and n == 0):
                    sp.wait_ge(zt_done, n * 4 + (2 * par - 2))
                sp.dma_start(z[par][:, NPAIR:DIN], dense[bass.ds(t * P, P), :]).then_inc(dense_in[par], 16)

            load_rows(0, 0)
            load_rows(0, 1)
            for c in range(WCH):
                if c >= 2:
                    sp.wait_ge(w_split, c - 1)
                for q in range(4):
                    sp.dma_start(stage[c % 2][32 * q:32 * q + 32, :],
                                 args["w_bil"][:, c * wcols:(c + 1) * wcols]).then_inc(w_staged[c % 2], 16)
            sp.dma_start(w1[:, 0:KC - 1, :], args["w1"][0:(KC - 1) * P, :].rearrange("(k p) n -> p k n", p=P)
                         ).then_inc(consts_in, 16)
            sp.dma_start(w1[0:KLAST, KC - 1, :], args["w1"][(KC - 1) * P:DIN, :]).then_inc(consts_in, 16)
            sp.dma_start(w2[:, :, :], args["W_top2"].rearrange("(k p) n -> p k n", p=P)).then_inc(consts_in, 16)
            sp.dma_start(w3[:, :], args["w3"]).then_inc(consts_in, 16)
            sp.dma_start(b1[:, :], args["b1"]).then_inc(consts_in, 16)
            sp.dma_start(b2[:, :], args["b2"]).then_inc(consts_in, 16)
            with sp.Fori(1, TILES // 2) as n:
                load_rows(n, 0)
                load_rows(n, 1)

        @block.gpsimd
        def _(pool):
            def gather(n, par, first):
                pool.wait_ge(idx_in[par], n * 16 + 16)
                pool.sem_inc(gather_may_start, 1)
                for g in range(NL):
                    if not first:
                        pool.wait_ge(prod_done, n * (2 * ns) + ((par - 2) * ns + plan.load_last[g] + 1))
                        pool.sem_inc(gather_may_start, 1)
                    for f in range(LF * g, LF * g + LF):
                        pool.indirect_dma_start(
                            out=emb[par][:, f * E:(f + 1) * E], out_offset=None, in_=tables[f],
                            in_offset=bass.IndirectOffsetOnAxis(ap=idx[par][:, f:f + 1], axis=0),
                        ).then_inc(gathered[par][g], 16)

            gather(0, 0, True)
            gather(0, 1, True)
            with pool.Fori(1, TILES // 2) as n:
                gather(n, 0, False)
                gather(n, 1, False)

        @block.scalar
        def _(act):
            act.dma_start(ident[:, :], args["ident"]).then_inc(consts_in, 16)
            for c in range(WCH):
                act.wait_ge(w_staged[c % 2], 64 * (c // 2 + 1))
                act.copy(w_stack[:, c * wcols:(c + 1) * wcols], stage[c % 2]).then_inc(w_rounded, 1)

            def step(s, n, par, prev, this, nxt):
                live = {-1: prev, 0: this, 1: nxt}
                for (q, g), dt in plan.hi_at.get(s, []):
                    if not live[dt]:
                        continue
                    buf, turn = (par + dt) % 2, (par + dt) // 2
                    lg = g * GF // LF
                    act.wait_ge(gathered[buf][lg], n * (LF * 16) + (turn + 1) * (LF * 16))
                    k = (2 * n + par + dt) * NG + q
                    if not (isinstance(k, int) and k < SRING):
                        act.wait_ge(stack_tr, k - SRING + 1)
                    x = emb[buf][:, g * GF * E:(g + 1) * GF * E].rearrange("p (f o e) -> p f o e", o=1, e=E)
                    act.copy(split[:, q_slot(par + dt, q), :, :, 0, :].bitcast(F32R),
                             x.to_broadcast([P, GF, 2, E])).then_inc(hi_done, 1)
                for (q, g), dt in plan.dup_at.get(s, []):
                    if not live[dt]:
                        continue
                    act.wait_ge(lo_done, (2 * n + par + dt) * NG + (q + 1))
                    part = split[:, q_slot(par + dt, q), :, :, 1, :]
                    act.copy(part[:, :, 1, :], part[:, :, 0, :]).then_inc(dup_done, 1)
                for (q, g), dt in plan.tr_at.get(s, []):
                    if not live[dt]:
                        continue
                    act.wait_ge(stack_tr, (2 * n + par + dt) * NG + (q + 1))
                    act.copy(x_stack[:, g * GF * P:(g + 1) * GF * P], stack_ps[:, :]).then_inc(stack_ready, 1)
                for (k, lo, hi), dt in plan.sum_at.get(s, []):
                    if hi < E or not live[dt]:
                        continue
                    act.wait_ge(bsum_done, (2 * n + par + dt) * nblk + (k + 1))
                    a, m = plan.blk_z[k], plan.blk_n[k]
                    act.copy(z[(par + dt) % 2][:, a:a + m], sum_ps[:, 0:m]).then_inc(bsum_saved, 1)
                for what, part in plan.mlp_at.get(s, []):
                    if not prev:
                        continue
                    t = 2 * n + (par - 1)
                    if what == "zt" and part == 0:
                        act.wait_ge(zt_done, t * 2 + 1)
                        act.copy(zt[:, 0:4, :].rearrange("p k b -> p (k b)"), zt_ps[:, 0:4 * P]).then_inc(zt_saved, 1)
                    elif what == "zt":
                        act.wait_ge(zt_done, t * 2 + 2)
                        act.copy(zt[:, 4:KC - 1, :].rearrange("p k b -> p (k b)"),
                                 zt_ps[:, 0:(KC - 5) * P]).then_inc(zt_saved, 1)
                        act.copy(zt[0:KLAST, KC - 1, :], zt_ps[0:KLAST, (KC - 5) * P:(KC - 4) * P]).then_inc(zt_saved, 1)
                    elif what == "h1" and part == (M1 - 1, 4, KC):
                        act.wait_ge(h1_done, t + 1)
                        for m in range(M1):
                            act.activation(h1t[:, m, :], h_ps[:, m * P:(m + 1) * P], ACT.Relu,
                                           bias=b1[:, m:m + 1]).then_inc(h1_saved, 1)
                    elif what == "h2" and part == M2 - 1:
                        act.wait_ge(h2_done, t + 1)
                        for m in range(M2):
                            act.activation(h2t[:, m, :], zt_ps[:, m * P:(m + 1) * P], ACT.Relu,
                                           bias=b2[:, m:m + 1]).then_inc(h2_saved, 1)
                    elif what == "y":
                        act.wait_ge(y_done, t + 1)
                        if not (isinstance(t, int) and t == 0):
                            act.wait_ge(y_stored, t * 16)
                        act.copy(y_row[:, :], h_ps[0:1, 0:P]).then_inc(y_saved, 1)
                        act.wait_ge(y_saved, t + 1)
                        act.dma_start(out_rows[bass.ds(t, 1), :], y_row[:, :]).then_inc(y_stored, 16)

            walk(act, step)
            act.wait_ge(y_stored, 16 * TILES)

        @block.vector
        def _(dve):
            for c in range(WCH):
                dve.wait_ge(w_staged[c % 2], 64 * (c // 2 + 1))
                dve.wait_ge(w_rounded, c + 1)
                cols = w_stack[64:128, c * wcols:(c + 1) * wcols]
                dve.tensor_tensor(cols, stage[c % 2][64:128, :], cols.bitcast(F32), ALU.subtract).then_inc(w_split, 1)

            def step(s, n, par, prev, this, nxt):
                live = {-1: prev, 0: this, 1: nxt}
                t = 2 * n + par
                r = steps[s]
                if this:
                    for g in plan.load_first.get(s, []):
                        dve.wait_ge(gathered[par][g], n * (LF * 16) + LF * 16)
                    dve.wait_ge(t_ready, t * ns + (s + 1))
                    if r.kind == "P":
                        k = r.block
                        done = t * nblk + (k - 1)
                        if s == plan.blk_first[k] and not (isinstance(done, int) and done <= 0):
                            dve.wait_ge(bsum_done, done)
                        off = r.z - plan.blk_z[k]
                        dst = prod_blk[k % 2][:, :, off:off + r.n].rearrange("p e (two n) -> p two n e", two=2)
                        dve.tensor_tensor(dst, t_pairs(r, s), emb_pairs(r, par), ALU.mult).then_inc(prod_done, 1)
                    else:
                        k = plan.d_index[s]
                        done = t * nd + (k - DRING + 1)
                        if not (isinstance(done, int) and done <= 0):
                            dve.wait_ge(dsum_done, done)
                        dst = prod_d[:, k % DRING, 0:r.n * E]
                        if r.diag:
                            dst = dst.rearrange("p (n e) -> p n e", e=E)
                        else:
                            dst = dst.rearrange("p (two n e) -> p two n e", two=2, e=E)
                        dve.tensor_tensor(dst, t_pairs(r, s), emb_pairs(r, par), ALU.mult).then_inc(prod_done, 1)
                b, dt = (s - 1, 0) if s else (ns - 1, -1)
                if live[dt] and steps[b].kind == "D":
                    rb, k = steps[b], plan.d_index[b]
                    if k == 0 and not (isinstance(n, int) and t + dt < 2):
                        dve.wait_ge(zt_done, (t + dt) * 2 - 2)
                    dve.wait_ge(prod_done, (t + dt) * ns + (b + 1))
                    dve.tensor_reduce(z[(par + dt) % 2][:, rb.z:rb.z + rb.n],
                                      prod_d[:, k % DRING, 0:rb.n * E].rearrange("p (n e) -> p n e", e=E),
                                      AX.X, ALU.add).then_inc(dsum_done, 1)
                for (q, g), dt in plan.lo_at.get(s, []):
                    if not live[dt]:
                        continue
                    buf = (par + dt) % 2
                    dve.wait_ge(hi_done, (t + dt) * NG + (q + 1))
                    part = split[:, q_slot(par + dt, q), :, 0, :, :]
                    dve.tensor_tensor(part[:, :, 1, :],
                                      emb[buf][:, g * GF * E:(g + 1) * GF * E].rearrange("p (f e) -> p f e", e=E),
                                      part[:, :, 0, :], ALU.subtract).then_inc(lo_done, 1)

            walk(dve, step)

        @block.tensor
        def _(pe):
            pe.wait_ge(consts_in, 16 * 7)

            def step(s, n, par, prev, this, nxt):
                live = {-1: prev, 0: this, 1: nxt}
                t = 2 * n + par
                for (q, g), dt in plan.tr_at.get(s, []):
                    if not live[dt]:
                        continue
                    k = (t + dt) * NG + q
                    pe.wait_ge(dup_done, k + 1)
                    if not (isinstance(k, int) and k == 0):
                        pe.wait_ge(stack_ready, k)
                    for f in range(GF):
                        a = split[:, q_slot(par + dt, q), f, :, :, :].rearrange("p c h e -> p (c h e)")
                        m = pe.transpose(stack_ps[:, f * P:(f + 1) * P], a, ident[:, :])
                    m.then_inc(stack_tr, 1)
                if this:
                    r = steps[s]
                    if isinstance(n, int) and n == 0 and par == 0 and s == 0:
                        pe.wait_ge(w_split, WCH)
                    qmax = max(plan.group_order.index(i // GF) for i in r.ii)
                    pe.wait_ge(stack_ready, t * NG + (qmax + 1))
                    if not (isinstance(n, int) and t * ns + s < 2):
                        pe.wait_ge(prod_done, t * ns + (s - 1))
                    for x, i in enumerate(r.ii):
                        nj = 1 if r.diag else r.nj
                        col = (x if r.diag else 0) * E + (0 if r.diag else x) * BANK
                        m = pe.matmul(t_ps[:, s % 2, col:col + nj * E], x_stack[:, i * P:(i + 1) * P],
                                      w_stack[:, (r.z + x * nj) * E:(r.z + (x + 1) * nj) * E],
                                      start=True, stop=True)
                    m.then_inc(t_ready, 1)
                for (k, lo, hi), dt in plan.sum_at.get(s, []):
                    if not live[dt]:
                        continue
                    if lo == 0:
                        pe.wait_ge(prod_done, (t + dt) * ns + (plan.blk_last[k] + 1))
                        done = (t + dt) * nblk + k
                        if not (isinstance(done, int) and done <= 0):
                            pe.wait_ge(bsum_saved, done)
                    for e in range(lo, hi):
                        m = pe.matmul(sum_ps[:, 0:plan.blk_n[k]], ident[:, :], prod_blk[k % 2][:, e, 0:plan.blk_n[k]],
                                      start=(e == 0), stop=(e == E - 1))
                    if hi == E:
                        m.then_inc(bsum_done, 1)
                for what, part in plan.mlp_at.get(s, []):
                    if not prev:
                        continue
                    u = 2 * n + (par - 1)
                    q = (par - 1) % 2
                    if what == "zt":
                        if part == 0:
                            pe.wait_ge(dsum_done, u * nd + nd)
                            pe.wait_ge(bsum_saved, u * nblk + nblk)
                            pe.wait_ge(dense_in[q], n * 16 + ((par - 1) // 2) * 16 + 16)
                            if not (isinstance(n, int) and u == 0):
                                pe.wait_ge(h2_saved, u * M2)
                        else:
                            pe.wait_ge(zt_saved, u * 3 + 1)
                        for c in range(4) if part == 0 else range(4, KC):
                            w = P if c < KC - 1 else KLAST
                            m = pe.transpose(zt_ps[0:w, (c % 4) * P:(c % 4 + 1) * P], z[q][:, c * P:c * P + w],
                                             ident[:, :])
                        m.then_inc(zt_done, 1)
                    elif what == "h1":
                        j, lo, hi = part
                        if j == 0 and lo == 0:
                            pe.wait_ge(zt_saved, u * 3 + 3)
                            if not (isinstance(n, int) and u == 0):
                                pe.wait_ge(y_saved, u)
                        for c in range(lo, hi):
                            w = P if c < KC - 1 else KLAST
                            m = pe.matmul(h_ps[:, j * P:(j + 1) * P], w1[0:w, c, j * P:(j + 1) * P], zt[0:w, c, :],
                                          start=(c == 0), stop=(c == KC - 1))
                        if part == (M1 - 1, 4, KC):
                            m.then_inc(h1_done, 1)
                    elif what == "h2":
                        if part == 0:
                            pe.wait_ge(h1_saved, u * M1 + M1)
                        for c in range(M1):
                            m = pe.matmul(zt_ps[:, part * P:(part + 1) * P], w2[:, c, part * P:(part + 1) * P],
                                          h1t[:, c, :], start=(c == 0), stop=(c == M1 - 1))
                        if part == M2 - 1:
                            m.then_inc(h2_done, 1)
                    elif what == "y":
                        pe.wait_ge(h2_saved, u * M2 + M2)
                        for c in range(M2):
                            m = pe.matmul(h_ps[0:1, 0:P], w3[:, c:c + 1], h2t[:, c, :],
                                          start=(c == 0), stop=(c == M2 - 1))
                        m.then_inc(y_done, 1)

            walk(pe, step)


def kernel(**inputs):
    from concourse import bacc
    from concourse.bass_utils import run_bass_kernel_spmd

    plan = Plan()
    rows = [i * (2 * NF - i - 1) // 2 + (j - i - 1) for i, j in plan.pairs]
    w_top1 = np.asarray(inputs["W_top1"])
    w_bil = np.asarray(inputs["L0_rec_bilinear_matrices"])
    host = {
        "dense_ctx": np.asarray(inputs["dense_ctx"]),
        "ids": np.asarray(inputs["ids"]),
        "w_bil": np.ascontiguousarray(w_bil[rows].transpose(1, 0, 2).reshape(E, NPAIR * E)),
        "w1": np.ascontiguousarray(w_top1[rows + list(range(NPAIR, DIN))]),
        "W_top2": np.asarray(inputs["W_top2"]),
        "w3": np.ascontiguousarray(np.asarray(inputs["W_top3"]).reshape(M2, P).T),
        "b1": np.ascontiguousarray(np.asarray(inputs["b_top1"]).reshape(M1, P).T),
        "b2": np.ascontiguousarray(np.asarray(inputs["b_top2"]).reshape(M2, P).T),
        "ident": np.eye(P, dtype=np.float32),
    }
    for f in range(NF):
        host[f"tbl_{f}"] = np.asarray(inputs[f"tbl_{f}"])

    nc = bacc.Bacc("TRN2", target_bir_lowering=False, num_devices=1)
    arrays, args = {}, {}
    for name, a in host.items():
        a = np.ascontiguousarray(a)
        arrays[f"in_{name}"] = a
        args[name] = nc.dram_tensor(f"in_{name}", a.shape, mybir.dt.from_np(a.dtype), kind="ExternalInput").ap()
    out = nc.dram_tensor("out_y", (B, 1), F32, kind="ExternalOutput").ap()
    build_tower(nc, args, out)
    r = run_bass_kernel_spmd(nc, [arrays], core_ids=[0])
    return r.results[0]["out_y"]
```

```python
from contextlib import ExitStack

import numpy as np

import concourse.bass as bass
from concourse import mybir

F32 = mybir.dt.float32
F32R = mybir.dt.float32r
I32 = mybir.dt.int32
ALU = mybir.AluOpType
ACT = mybir.ActivationFunctionType
AX = mybir.AxisListType

NF = 40
E = 32
B = 2048
P = 128
TILES = B // P
NPAIR = NF * (NF - 1) // 2
DENSE = 16
H1, H2 = 512, 256
DIN = NPAIR + DENSE
BANK = 512
RUN = BANK // E
FAST = 256
GF = 8
NG = NF // GF
M1, M2 = H1 // P, H2 // P
DRING = 2
SRING = 2


class Region:

    def __init__(self, b, j0=0, nj=0):
        self.b, self.j0, self.nj = b, j0, nj
        self.tail = b is None
        self.ii = [NF - 1] if self.tail else [2 * b, 2 * b + 1]
        self.n = NF // 2 if self.tail else 2 * nj
        self.kind = None
        self.z = self.w = None
        self.block = None
        self.off = None

    def pairs(self):
        if self.tail:
            return [(NF - 1, j) for j in range(0, NF, 2)]
        return [(i, self.j0 + x + k) for x, i in enumerate(self.ii) for k in range(self.nj)]


class Plan:

    LEAD = 4
    DSHARE = 0.17
    H1_EVERY = 2
    PASS = 110

    def __init__(self):
        steps, made_d, made = [], 0, 0
        room, blk = P, 0
        self.blk_n = [0]
        for b in range(NF // 2 - 2, -1, -1):
            total = NF - 2 - 2 * b
            runs = -(-total // RUN)
            j = 2 * b + 1
            for c in range(runs):
                nj = total // runs + (c < total % runs)
                made += 2 * nj
                if made_d + nj < self.DSHARE * made:
                    r = Region(b, j, nj)
                    r.kind = "D"
                    made_d += 2 * nj
                    steps.append(r)
                    j += nj
                    continue
                while nj:
                    if room < 8:
                        blk, room = blk + 1, P
                        self.blk_n.append(0)
                    m = min(nj, room // 2)
                    r = Region(b, j, m)
                    r.kind, r.block, r.off = "P", blk, P - room
                    self.blk_n[blk] += 2 * m
                    steps.append(r)
                    room -= 2 * m
                    j += m
                    nj -= m
        r = Region(None)
        r.kind = "D"
        steps.insert(len(steps) - 1, r)
        self.steps = steps
        self.ns = ns = len(steps)
        self.nblk = len(self.blk_n)
        self.nd = sum(r.kind == "D" for r in steps)
        self.blk_z = [sum(self.blk_n[:k]) for k in range(self.nblk)]
        self.blk_first = [min(s for s, r in enumerate(steps) if r.block == k) for k in range(self.nblk)]
        self.blk_last = [max(s for s, r in enumerate(steps) if r.block == k) for k in range(self.nblk)]
        z = self.zd = sum(self.blk_n)
        for r in sorted((r for r in steps if r.kind == "D"), key=lambda r: r.n):
            r.z = z
            z += r.n
        w = 0
        for r in steps:
            if r.kind == "P":
                r.z = self.blk_z[r.block] + r.off
            r.w = w
            w += r.n
        assert z == NPAIR
        self.nz = NPAIR - self.zd
        self.pairs = [None] * NPAIR
        for r in steps:
            for k, pr in enumerate(r.pairs()):
                self.pairs[r.z + k] = pr
        self.w_pairs = [pr for r in steps for pr in r.pairs()]
        assert sorted((min(p), max(p)) for p in self.pairs) == [(i, j) for i in range(NF) for j in range(i + 1, NF)]
        self.d_index = {s: k for k, s in enumerate(s for s, r in enumerate(steps) if r.kind == "D")}
        self.kchunks = list(zip(self.blk_z, self.blk_n))
        for a in range(self.zd, DIN, P):
            self.kchunks.append((a, min(P, DIN - a)))
        self.kc = len(self.kchunks)
        self.kz = self.kc - self.nblk
        first = [min(s for s, r in enumerate(steps) if not r.tail and any(i // GF == g for i in r.ii)) for g in range(NG)]
        last = [max(s for s, r in enumerate(steps) if not r.tail and any(i // GF == g for i in r.ii)) for g in range(NG)]
        self.order = sorted(range(NG), key=lambda g: first[g])
        at, nxt = {}, 10 ** 9
        for g in reversed(self.order):
            at[g] = min(first[g] - self.LEAD, nxt - 5)
            nxt = at[g]
        self.tr_at, self.hi_at, self.lo_at = {}, {}, {}
        for q, g in enumerate(self.order):
            a = at[g]
            assert a + ns > last[g] or g == NG - 1
            self.put(self.tr_at, a, (q, g))
            self.put(self.hi_at, a - 4, (q, g))
            self.put(self.lo_at, a - 3, (q, g))
        zt_step = self.blk_last[0] + 1
        h1_step = zt_step + 4
        halves = [(m, lo, hi) for m in range(M1) for lo, hi in ((0, self.kc // 2), (self.kc // 2, self.kc))]
        self.mlp_at = {zt_step: [("zt", None)]}
        for x, part in enumerate(halves):
            self.mlp_at[h1_step + self.H1_EVERY * x] = [("h1", part)]
        m = h1_step + self.H1_EVERY * (len(halves) - 1) + 2
        self.mlp_at.setdefault(m, []).append(("h2", 0))
        self.mlp_at.setdefault(m + 1, []).append(("h2", 1))
        self.mlp_at.setdefault(m + 3, []).append(("y", None))
        assert max(self.mlp_at) < ns
        dve = [(1 if r.kind == "P" else 2) * (r.n * E + 64) for r in steps]
        pe = [r.n * E * 0.4 for r in steps]
        for s_, v in self.tr_at.items():
            pe[s_] += len(v) * GF // 2 * self.PASS
        for s_, v in self.mlp_at.items():
            for what, part in v:
                pe[s_] += {"zt": 2, "h1": self.kc, "h2": 2 * M1, "y": 2 * M2}[what] * self.PASS
        self.sum_at, self.sum_end = {}, {}
        for k in range(self.nblk):
            a = self.blk_last[k] + 2
            b = (self.blk_last[k + 1] if k + 1 < self.nblk else ns + self.blk_last[0]) + 1
            lo, hi = 0.0, 9.0
            for _ in range(40):
                mid = (lo + hi) / 2
                w = [max(0.0, mid * dve[x % ns] - pe[x % ns]) for x in range(a, b)]
                lo, hi = (mid, hi) if sum(w) < E * self.PASS else (lo, mid)
            done = 0
            for x in range(a, b):
                end = E if x == b - 1 else round(E * sum(w[:x - a + 1]) / sum(w))
                if end > done:
                    self.put(self.sum_at, x, (k, done, end))
                    if end == E:
                        self.sum_end[k] = x
                done = end
        assert self.sum_end[self.nblk - 1] - ns < h1_step - 1

        self.load_first, self.load_last = {}, []
        for k in range(NG):
            uses = [s for s, r in enumerate(steps) if any(j // GF == k for _, j in r.pairs())]
            self.load_first.setdefault(min(uses), []).append(k)
            split = [x + 1 - dt * ns for x, v in self.lo_at.items() for (q, g), dt in v if g == k]
            self.load_last.append(max(uses + split))
        assert max(self.load_last) < ns

    def put(self, table, s, what):
        dt = -(s // self.ns)
        table.setdefault(s % self.ns, []).append((what, dt))


def build_tower(nc, args, out):
    plan = Plan()
    steps, ns, nd, nblk = plan.steps, plan.ns, plan.nd, plan.nblk
    kc, kz = plan.kc, plan.kz
    ndmax = max(r.n for r in steps if r.kind == "D")
    tables = [args[f"tbl_{f}"] for f in range(NF)]
    ids, dense = args["ids"], args["dense_ctx"]
    out_rows = out.rearrange("(t b) o -> t (o b)", b=P)

    with ExitStack() as ctx:
        def sb(name, shape, dt=F32):
            return ctx.enter_context(nc.sbuf_tensor(name, shape, dt))

        def psum(name, shape, dt=F32):
            return ctx.enter_context(nc.psum_tensor(name, shape, dt))

        def sem(name):
            return ctx.enter_context(nc.semaphore(name))

        w_stack = sb("w_stack", [P, NPAIR * E], F32R)
        x_stack = sb("x_stack", [P, (NF + GF) * P], F32R)
        prod_blk = [sb(f"prod_blk{k}", [P, E, P]) for k in range(2)]
        prod_d = sb("prod_d", [P, DRING, ndmax * E])
        emb = [sb(f"emb{k}", [P, NF * E]) for k in range(2)]
        split = sb("split", [P, SRING, GF, 2, E])
        idx = [sb(f"idx{k}", [P, NF], I32) for k in range(2)]
        z = [sb(f"z{k}", [P, plan.nz + DENSE]) for k in range(2)]
        zt = [sb(f"zt{k}", [P, kc, P]) for k in range(2)]
        h1t = sb("h1t", [P, M1, P])
        h2t = sb("h2t", [P, M2, P])
        y_row = sb("y_row", [1, P])
        w1 = sb("w1", [P, kc, H1])
        w2 = sb("w2", [P, M1, H2])
        w3 = sb("w3", [P, M2])
        b1 = sb("b1", [P, M1])
        b2 = sb("b2", [P, M2])
        ident = sb("ident", [P, P])

        t_ps = psum("t_ps", [P, 2, 2 * BANK])
        stack_ps = psum("stack_ps", [P, GF // 2 * P])
        sum_ps = psum("sum_ps", [P, BANK])[:, 0:P]
        zt_ps = psum("zt_ps", [P, BANK])
        h_ps = psum("h_ps", [P, BANK])

        w_staged = [sem(f"w_staged{k}") for k in range(4)]
        w_rounded = sem("w_rounded")
        w_split = sem("w_split")
        consts_in = sem("consts_in")
        idx_in = [sem(f"idx_in{k}") for k in range(2)]
        dense_in = [sem(f"dense_in{k}") for k in range(2)]
        gathered = [[sem(f"gathered{k}_{g}") for g in range(NG)] for k in range(2)]
        gather_may_start = sem("gather_may_start")
        hi_done = sem("hi_done")
        lo_done = sem("lo_done")
        stack_tr = sem("stack_tr")
        stack_ready = sem("stack_ready")
        t_ready = sem("t_ready")
        prod_done = sem("prod_done")
        dsum_done = sem("dsum_done")
        bsum_done = sem("bsum_done")
        bsum_saved = sem("bsum_saved")
        zt_done = sem("zt_done")
        zt_saved = sem("zt_saved")
        h1_done = sem("h1_done")
        h1_saved = sem("h1_saved")
        h2_done = sem("h2_done")
        h2_saved = sem("h2_saved")
        y_done = sem("y_done")
        y_saved = sem("y_saved")
        y_stored = sem("y_stored")

        WCH = 16
        WBUF = 4
        wcols = NPAIR * E // WCH
        assert 2 * wcols <= E * P and wcols * WCH == NPAIR * E
        halves = [b[:].rearrange("p e n -> p (e n)") for b in prod_blk]
        stage = [halves[k // 2][:, k % 2 * wcols:(k % 2 + 1) * wcols] for k in range(WBUF)]

        def field(buf, g0, g1):
            return emb[buf][:, g0 * E:g1 * E].rearrange("p (f e) -> p f e", e=E)

        def t_slot(par, s):
            return ((par % 2) * ns + s) % 2

        def pairs_of(r, buf, half):
            if r.tail:
                xj = emb[buf][:, :].rearrange("p (b two e) -> p b two e", two=2, e=E)[:, :, 0, :]
                return t_ps[:, half, 0:r.n * E].rearrange("p (n e) -> p n e", e=E), xj
            w = emb[buf][:, r.j0 * E:(r.j0 + r.nj) * E]
            xj = bass.AP(w.tensor, w.offset, [list(w.ap[0]), [E, 2], [E, r.nj], [1, E]])
            t = t_ps[:, half, :].rearrange("p (two n e) -> p two n e", two=2, e=E)
            return t[:, :, 0:r.nj, :], xj

        def x_col(i, par):
            return (i + (GF if i >= NF - GF and par % 2 else 0)) * P

        def q_slot(par, q):
            return ((par % 2) * NG + q) % SRING

        assert 2 * NG % SRING == 0 and 2 * nd % DRING == 0 and 2 * nblk % 2 == 0

        def walk(engine, step):
            last = TILES // 2 - 1
            for s in range(ns):
                step(s, -1, 1, False, False, True)
            for par in range(2):
                for s in range(ns):
                    step(s, 0, par, par > 0, True, True)
            with engine.Fori(1, last) as n:
                for par in range(2):
                    for s in range(ns):
                        step(s, n, par, True, True, True)
            for par in range(2):
                for s in range(ns):
                    step(s, last, par, True, True, par == 0)
            for s in range(ns):
                step(s, last + 1, 0, True, False, False)

        block = ctx.enter_context(nc.Block())

        @block.sync
        def _(sp):
            def load_rows(n, par):
                t = 2 * n + par
                for g in range(NG):
                    if not (isinstance(n, int) and n == 0):
                        sp.wait_ge(gathered[par][g], n * (GF * 16))
                sp.dma_start(idx[par][:, :], ids[bass.ds(t * P, P), :]).then_inc(idx_in[par], 16)
                if not (isinstance(n, int) and n == 0):
                    sp.wait_ge(zt_done, n * 2 + (par - 1))
                sp.dma_start(z[par][:, plan.nz:plan.nz + DENSE], dense[bass.ds(t * P, P), :]).then_inc(dense_in[par], 16)

            load_rows(0, 0)
            load_rows(0, 1)
            for c in range(WCH):
                if c >= WBUF:
                    sp.wait_ge(w_split, c - WBUF + 1)
                for q in range(4):
                    sp.dma_start(stage[c % WBUF][32 * q:32 * q + 32, :],
                                 args["w_bil"][:, c * wcols:(c + 1) * wcols]).then_inc(w_staged[c % WBUF], 16)
            for c, (a, m) in enumerate(plan.kchunks):
                sp.dma_start(w1[0:m, c, :], args["w1"][a:a + m, :]).then_inc(consts_in, 16)
            sp.dma_start(w2[:, :, :], args["W_top2"].rearrange("(k p) n -> p k n", p=P)).then_inc(consts_in, 16)
            sp.dma_start(w3[:, :], args["w3"]).then_inc(consts_in, 16)
            sp.dma_start(b1[:, :], args["b1"]).then_inc(consts_in, 16)
            sp.dma_start(b2[:, :], args["b2"]).then_inc(consts_in, 16)
            with sp.Fori(1, TILES // 2) as n:
                load_rows(n, 0)
                load_rows(n, 1)

        @block.gpsimd
        def _(pool):
            def gather(n, par, first):
                pool.wait_ge(idx_in[par], n * 16 + 16)
                pool.sem_inc(gather_may_start, 1)
                for g in plan.order:
                    if not first:
                        pool.wait_ge(prod_done, n * (2 * ns) + ((par - 2) * ns + plan.load_last[g] + 1))
                        pool.sem_inc(gather_may_start, 1)
                    for f in range(GF * g, GF * g + GF):
                        pool.indirect_dma_start(
                            out=emb[par][:, f * E:(f + 1) * E], out_offset=None, in_=tables[f],
                            in_offset=bass.IndirectOffsetOnAxis(ap=idx[par][:, f:f + 1], axis=0),
                        ).then_inc(gathered[par][g], 16)

            gather(0, 0, True)
            gather(0, 1, True)
            with pool.Fori(1, TILES // 2) as n:
                gather(n, 0, False)
                gather(n, 1, False)

        @block.scalar
        def _(act):
            act.dma_start(ident[:, :], args["ident"]).then_inc(consts_in, 16)
            for c in range(WCH):
                act.wait_ge(w_staged[c % WBUF], 64 * (c // WBUF + 1))
                act.copy(w_stack[:, c * wcols:(c + 1) * wcols], stage[c % WBUF]).then_inc(w_rounded, 1)

            def step(s, n, par, prev, this, nxt):
                live = {-1: prev, 0: this, 1: nxt}
                for (q, g), dt in plan.hi_at.get(s, []):
                    if not live[dt]:
                        continue
                    buf, turn = (par + dt) % 2, (par + dt) // 2
                    act.wait_ge(gathered[buf][g], n * (GF * 16) + (turn + 1) * (GF * 16))
                    k = (2 * n + par + dt) * NG + q
                    if not (isinstance(k, int) and k < SRING):
                        act.wait_ge(stack_tr, k - SRING + 1)
                    act.copy(split[:, q_slot(par + dt, q), :, 0, :].bitcast(F32R),
                             field(buf, g * GF, g * GF + GF)).then_inc(hi_done, 1)
                for (q, g), dt in plan.tr_at.get(s, []):
                    if not live[dt]:
                        continue
                    act.wait_ge(stack_tr, (2 * n + par + dt) * NG + (q + 1))
                    a = x_col(g * GF, par + dt)
                    stacks = x_stack[:, a:a + GF * P].rearrange("k (f two b) -> k f two b", two=2, b=P)
                    for odd in range(2):
                        for half in range(2):
                            act.copy(stacks[64 * half:64 * half + 64, :, odd, :],
                                     stack_ps[64 * odd:64 * odd + 64, :].rearrange("k (f b) -> k f b", b=P)
                                     ).then_inc(stack_ready, 1)
                for (k, lo, hi), dt in plan.sum_at.get(s, []):
                    if hi < E or not live[dt]:
                        continue
                    act.wait_ge(bsum_done, (2 * n + par + dt) * nblk + (k + 1))
                    act.copy(zt[(par + dt) % 2][0:plan.blk_n[k], k, :], sum_ps[0:plan.blk_n[k], :]).then_inc(bsum_saved, 1)
                for what, part in plan.mlp_at.get(s, []):
                    if not prev:
                        continue
                    t = 2 * n + (par - 1)
                    if what == "zt":
                        act.wait_ge(zt_done, t + 1)
                        for c in range(nblk, kc):
                            m = plan.kchunks[c][1]
                            act.copy(zt[(par - 1) % 2][0:m, c, :],
                                     zt_ps[0:m, (c - nblk) * P:(c - nblk + 1) * P]).then_inc(zt_saved, 1)
                    elif what == "h1" and part == (M1 - 1, kc // 2, kc):
                        act.wait_ge(h1_done, t + 1)
                        for m in range(M1):
                            act.activation(h1t[:, m, :], h_ps[:, m * P:(m + 1) * P], ACT.Relu,
                                           bias=b1[:, m:m + 1]).then_inc(h1_saved, 1)
                    elif what == "h2" and part == M2 - 1:
                        act.wait_ge(h2_done, t + 1)
                        for m in range(M2):
                            act.activation(h2t[:, m, :], zt_ps[:, m * P:(m + 1) * P], ACT.Relu,
                                           bias=b2[:, m:m + 1]).then_inc(h2_saved, 1)
                    elif what == "y":
                        act.wait_ge(y_done, t + 1)
                        if not (isinstance(t, int) and t == 0):
                            act.wait_ge(y_stored, t * 16)
                        act.copy(y_row[:, :], h_ps[0:1, 0:P]).then_inc(y_saved, 1)
                        act.wait_ge(y_saved, t + 1)
                        act.dma_start(out_rows[bass.ds(t, 1), :], y_row[:, :]).then_inc(y_stored, 16)

            walk(act, step)
            act.wait_ge(y_stored, 16 * TILES)

        @block.vector
        def _(dve):
            for c in range(WCH):
                dve.wait_ge(w_staged[c % WBUF], 64 * (c // WBUF + 1))
                dve.wait_ge(w_rounded, c + 1)
                cols = w_stack[64:128, c * wcols:(c + 1) * wcols]
                dve.tensor_tensor(cols, stage[c % WBUF][64:128, :], cols.bitcast(F32), ALU.subtract).then_inc(w_split, 1)

            def step(s, n, par, prev, this, nxt):
                live = {-1: prev, 0: this, 1: nxt}
                t = 2 * n + par
                r = steps[s]
                if this:
                    for g in plan.load_first.get(s, []):
                        dve.wait_ge(gathered[par][g], n * (GF * 16) + GF * 16)
                    dve.wait_ge(t_ready, t * ns + (s + 1))
                    tv, xj = pairs_of(r, par, t_slot(par, s))
                    if r.kind == "P":
                        k = r.block
                        done = t * nblk + (k - 1)
                        if s == plan.blk_first[k] and not (isinstance(done, int) and done <= 0):
                            dve.wait_ge(bsum_done, done)
                        dst = prod_blk[(par * nblk + k) % 2][:, :, r.off:r.off + r.n].rearrange(
                            "p e (two n) -> p two n e", two=2)
                        dve.tensor_tensor(dst, tv, xj, ALU.mult).then_inc(prod_done, 1)
                    else:
                        k = plan.d_index[s]
                        done = t * nd + (k - DRING + 1)
                        if not (isinstance(done, int) and done <= 0):
                            dve.wait_ge(dsum_done, done)
                        dst = prod_d[:, (par * nd + k) % DRING, 0:r.n * E]
                        if r.tail:
                            dst = dst.rearrange("p (n e) -> p n e", e=E)
                        else:
                            dst = dst.rearrange("p (two n e) -> p two n e", two=2, e=E)
                        dve.tensor_tensor(dst, tv, xj, ALU.mult).then_inc(prod_done, 1)
                b, dt = (s - 1, 0) if s else (ns - 1, -1)
                if live[dt] and steps[b].kind == "D":
                    rb, k = steps[b], plan.d_index[b]
                    if k == 0 and not (isinstance(n, int) and t + dt < 2):
                        dve.wait_ge(zt_done, (t + dt) - 1)
                    dve.wait_ge(prod_done, (t + dt) * ns + (b + 1))
                    dve.tensor_reduce(z[(par + dt) % 2][:, rb.z - plan.zd:rb.z - plan.zd + rb.n],
                                      prod_d[:, ((par + dt) * nd + k) % DRING, 0:rb.n * E].rearrange("p (n e) -> p n e", e=E),
                                      AX.X, ALU.add).then_inc(dsum_done, 1)
                for (q, g), dt in plan.lo_at.get(s, []):
                    if not live[dt]:
                        continue
                    buf = (par + dt) % 2
                    dve.wait_ge(hi_done, (t + dt) * NG + (q + 1))
                    part = split[:, q_slot(par + dt, q), :, :, :]
                    dve.tensor_tensor(part[:, :, 1, :], field(buf, g * GF, g * GF + GF), part[:, :, 0, :],
                                      ALU.subtract).then_inc(lo_done, 1)

            walk(dve, step)

        @block.tensor
        def _(pe):
            pe.wait_ge(consts_in, 16 * (kc + 5))

            def step(s, n, par, prev, this, nxt):
                live = {-1: prev, 0: this, 1: nxt}
                t = 2 * n + par
                for (q, g), dt in plan.tr_at.get(s, []):
                    if not live[dt]:
                        continue
                    k = (t + dt) * NG + q
                    pe.wait_ge(lo_done, k + 1)
                    if not (isinstance(k, int) and k == 0):
                        pe.wait_ge(stack_ready, k * 4)
                    for f in range(GF // 2):
                        a = split[:, q_slot(par + dt, q), 2 * f:2 * f + 2, :, :].rearrange("p f h e -> p (f h e)")
                        m = pe.transpose(stack_ps[:, f * P:(f + 1) * P], a, ident[:, :])
                    m.then_inc(stack_tr, 1)
                if this:
                    r = steps[s]
                    if isinstance(n, int) and n == 0 and par == 0 and s == 0:
                        pe.wait_ge(w_split, WCH)
                    q = max(plan.order.index(i // GF) for i in r.ii)
                    pe.wait_ge(stack_ready, t * (4 * NG) + (q + 1) * 4)
                    if not (isinstance(n, int) and t * ns + s < 2):
                        pe.wait_ge(prod_done, t * ns + (s - 1))
                    if r.tail:
                        runs = [(r.ii[0], a, min(RUN, r.n - a)) for a in range(0, r.n, RUN)]
                    else:
                        runs = [(i, x * r.nj, r.nj) for x, i in enumerate(r.ii)]
                    for x, (i, a, nj) in enumerate(runs):
                        cols = max(nj * E, FAST)
                        m = pe.matmul(t_ps[:, t_slot(par, s), x * BANK:x * BANK + cols],
                                      x_stack[:, x_col(i, par):x_col(i, par) + P],
                                      w_stack[:, (r.w + a) * E:(r.w + a) * E + cols], start=True, stop=True)
                    m.then_inc(t_ready, 1)
                for (k, lo, hi), dt in plan.sum_at.get(s, []):
                    if not live[dt]:
                        continue
                    if lo == 0:
                        pe.wait_ge(prod_done, (t + dt) * ns + (plan.blk_last[k] + 1))
                        done = (t + dt) * nblk + k
                        if not (isinstance(done, int) and done <= 0):
                            pe.wait_ge(bsum_saved, done)
                    m_blk = plan.blk_n[k]
                    for e in range(lo, hi):
                        m = pe.matmul(sum_ps[0:m_blk, :], prod_blk[((par + dt) * nblk + k) % 2][:, e, 0:m_blk],
                                      ident[:, :], start=(e == 0), stop=(e == E - 1), is_transpose=True)
                    if hi == E:
                        m.then_inc(bsum_done, 1)
                for what, part in plan.mlp_at.get(s, []):
                    if not prev:
                        continue
                    u = 2 * n + (par - 1)
                    q = (par - 1) % 2
                    if what == "zt":
                        pe.wait_ge(dsum_done, u * nd + nd)
                        pe.wait_ge(dense_in[q], n * 16 + ((par - 1) // 2) * 16 + 16)
                        if not (isinstance(n, int) and u == 0):
                            pe.wait_ge(h2_saved, u * M2)
                        for c in range(kz):
                            w = plan.kchunks[nblk + c][1]
                            m = pe.transpose(zt_ps[0:w, c * P:(c + 1) * P], z[q][:, c * P:c * P + w], ident[:, :])
                        m.then_inc(zt_done, 1)
                    elif what == "h1":
                        j, lo, hi = part
                        if part == (0, 0, kc // 2):
                            pe.wait_ge(zt_saved, u * kz + kz)
                            pe.wait_ge(bsum_saved, u * nblk + nblk)
                            if not (isinstance(n, int) and u == 0):
                                pe.wait_ge(y_saved, u)
                        for c in range(lo, hi):
                            w = plan.kchunks[c][1]
                            m = pe.matmul(h_ps[:, j * P:(j + 1) * P], w1[0:w, c, j * P:(j + 1) * P],
                                          zt[q][0:w, c, :], start=(c == 0), stop=(c == kc - 1))
                        if part == (M1 - 1, kc // 2, kc):
                            m.then_inc(h1_done, 1)
                    elif what == "h2":
                        pe.wait_ge(h1_saved, u * M1 + M1)
                        for c in range(M1):
                            m = pe.matmul(zt_ps[:, part * P:(part + 1) * P], w2[:, c, part * P:(part + 1) * P],
                                          h1t[:, c, :], start=(c == 0), stop=(c == M1 - 1))
                        if part == M2 - 1:
                            m.then_inc(h2_done, 1)
                    elif what == "y":
                        pe.wait_ge(h2_saved, u * M2 + M2)
                        for c in range(M2):
                            m = pe.matmul(h_ps[0:1, 0:P], w3[:, c:c + 1], h2t[:, c, :],
                                          start=(c == 0), stop=(c == M2 - 1))
                        m.then_inc(y_done, 1)

            walk(pe, step)


def kernel(**inputs):
    from concourse import bacc
    from concourse.bass_utils import run_bass_kernel_spmd

    plan = Plan()
    def numbers(pairs):
        return [min(p) * (2 * NF - min(p) - 1) // 2 + (max(p) - min(p) - 1) for p in pairs]

    w_top1 = np.asarray(inputs["W_top1"])
    w_bil = np.asarray(inputs["L0_rec_bilinear_matrices"])[numbers(plan.w_pairs)]
    swapped = np.array([i > j for i, j in plan.w_pairs])
    w_bil[swapped] = w_bil[swapped].transpose(0, 2, 1)
    host = {
        "dense_ctx": np.asarray(inputs["dense_ctx"]),
        "ids": np.asarray(inputs["ids"]),
        "w_bil": np.ascontiguousarray(w_bil.transpose(1, 0, 2).reshape(E, NPAIR * E)),
        "w1": np.ascontiguousarray(w_top1[numbers(plan.pairs) + list(range(NPAIR, DIN))]),
        "W_top2": np.asarray(inputs["W_top2"]),
        "w3": np.ascontiguousarray(np.asarray(inputs["W_top3"]).reshape(M2, P).T),
        "b1": np.ascontiguousarray(np.asarray(inputs["b_top1"]).reshape(M1, P).T),
        "b2": np.ascontiguousarray(np.asarray(inputs["b_top2"]).reshape(M2, P).T),
        "ident": np.eye(P, dtype=np.float32),
    }
    for f in range(NF):
        host[f"tbl_{f}"] = np.asarray(inputs[f"tbl_{f}"])

    nc = bacc.Bacc("TRN2", target_bir_lowering=False, num_devices=1)
    arrays, args = {}, {}
    for name, a in host.items():
        a = np.ascontiguousarray(a)
        arrays[f"in_{name}"] = a
        args[name] = nc.dram_tensor(f"in_{name}", a.shape, mybir.dt.from_np(a.dtype), kind="ExternalInput").ap()
    out = nc.dram_tensor("out_y", (B, 1), F32, kind="ExternalOutput").ap()
    build_tower(nc, args, out)
    r = run_bass_kernel_spmd(nc, [arrays], core_ids=[0])
    return r.results[0]["out_y"]
```

```python
from contextlib import ExitStack

import numpy as np

import concourse.bass as bass
from concourse import mybir

F32 = mybir.dt.float32
F32R = mybir.dt.float32r
I32 = mybir.dt.int32
ALU = mybir.AluOpType
ACT = mybir.ActivationFunctionType
AX = mybir.AxisListType

NF = 40
E = 32
B = 2048
P = 128
TILES = B // P
NPAIR = NF * (NF - 1) // 2
DENSE = 16
H1, H2 = 512, 256
DIN = NPAIR + DENSE
BANK = 512
RUN = BANK // E
FAST = 256
GF = 4
NG = NF // GF
M1, M2 = H1 // P, H2 // P
DRING = 2
SRING = 4
WCH = 32
WBUF = 4
WCOLS = NPAIR * E // WCH
TRING = 3
MLP = [("zt", 0)] + [("h1", m) for m in range(M1)] + [("h2", 0), ("y", 0)]
NMLP = len(MLP)


class Region:

    def __init__(self, b, j0=0, nj=0):
        self.b, self.j0, self.nj = b, j0, nj
        self.tail = b is None
        self.ii = [NF - 1] if self.tail else [2 * b, 2 * b + 1]
        self.n = NF // 2 if self.tail else 2 * nj
        self.kind = None
        self.z = self.w = None
        self.block = None
        self.off = None

    def runs(self):
        if self.tail:
            runs = [(NF - 1, a, min(RUN, self.n - a)) for a in range(0, self.n, RUN)]
        else:
            runs = [(i, x * self.nj, self.nj) for x, i in enumerate(self.ii)]
        return [(i, a * E, max(nj * E, FAST)) for i, a, nj in runs]

    def pairs(self):
        if self.tail:
            return [(NF - 1, j) for j in range(0, NF, 2)]
        return [(i, self.j0 + x + k) for x, i in enumerate(self.ii) for k in range(self.nj)]


class Plan:

    D_RUNS = (9, 16, 17, 20, 22)
    TAIL_AT = -12
    TR_AT = (-5, -2, -1, 2, 6, 8, 12, 18, 22, 27)
    MLP_AT = (4, 14, 19, 22, 24, 28, 35)
    SUM_TILT = (0.8, 1.9, 0.7, 4.8, -0.6)
    HI_LEAD = 3
    LO_LEAD = 3
    W_FIRST = 2
    W_AHEAD = 8
    W_SPAN = 29
    W_LEAD = 3
    PASS = 110

    def __init__(self):
        steps, run = [], 0
        blk, room = 0, P
        self.blk_n = [0]
        for b in range(NF // 2 - 2, -1, -1):
            total = NF - 2 - 2 * b
            runs = -(-total // RUN)
            j = 2 * b + 1
            for c in range(runs):
                nj = total // runs + (c < total % runs)
                run += 1
                if run - 1 in self.D_RUNS:
                    r = Region(b, j, nj)
                    r.kind = "D"
                    steps.append(r)
                    j += nj
                    continue
                while nj:
                    if room < 8:
                        blk, room = blk + 1, P
                        self.blk_n.append(0)
                    m = min(nj, room // 2)
                    r = Region(b, j, m)
                    r.kind, r.block, r.off = "P", blk, P - room
                    self.blk_n[blk] += 2 * m
                    steps.append(r)
                    room -= 2 * m
                    j += m
                    nj -= m
        r = Region(None)
        r.kind = "D"
        steps.insert(len(steps) + self.TAIL_AT, r)
        self.steps = steps
        self.ns = ns = len(steps)
        self.nblk = len(self.blk_n)
        self.nd = sum(r.kind == "D" for r in steps)
        self.blk_z = [sum(self.blk_n[:k]) for k in range(self.nblk)]
        self.blk_first = [min(s for s, r in enumerate(steps) if r.block == k) for k in range(self.nblk)]
        self.blk_last = [max(s for s, r in enumerate(steps) if r.block == k) for k in range(self.nblk)]
        z = self.zd = sum(self.blk_n)
        for r in sorted((r for r in steps if r.kind == "D"), key=lambda r: r.n):
            r.z = z
            z += r.n
        w = 0
        for r in steps:
            if r.kind == "P":
                r.z = self.blk_z[r.block] + r.off
            r.w = w
            w += r.n
        assert z == NPAIR
        self.nz = NPAIR - self.zd
        self.pairs = [None] * NPAIR
        for r in steps:
            for k, pr in enumerate(r.pairs()):
                self.pairs[r.z + k] = pr
        self.w_pairs = [pr for r in steps for pr in r.pairs()]
        assert sorted((min(p), max(p)) for p in self.pairs) == [(i, j) for i in range(NF) for j in range(i + 1, NF)]
        self.d_index = {s: k for k, s in enumerate(s for s, r in enumerate(steps) if r.kind == "D")}
        self.kchunks = list(zip(self.blk_z, self.blk_n))
        for a in range(self.zd, DIN, P):
            self.kchunks.append((a, min(P, DIN - a)))
        self.kc = len(self.kchunks)
        self.kz = self.kc - self.nblk
        first = [min(s for s, r in enumerate(steps) if not r.tail and any(i // GF == g for i in r.ii)) for g in range(NG)]
        last = [max(s for s, r in enumerate(steps) if not r.tail and any(i // GF == g for i in r.ii)) for g in range(NG)]
        self.order = sorted(range(NG), key=lambda g: first[g])
        self.tr_at, self.hi_at, self.lo_at = {}, {}, {}
        for q, g in enumerate(self.order):
            a = self.TR_AT[q]
            assert a < first[g]
            assert a + ns > last[g] or g == NG - 1
            self.put(self.tr_at, a, (q, g))
            self.put(self.hi_at, a - self.HI_LEAD, (q, g))
            self.put(self.lo_at, a - self.LO_LEAD, (q, g))
        counts = {"zt": self.kz, "h1": self.kc, "h2": M1 * M2, "y": M2}
        self.mlp_count = [counts[what] for what, _ in MLP]
        self.mlp_at = {}
        for x, (what, m) in enumerate(MLP):
            a = self.MLP_AT[x]
            nsteps = 2 if what in ("h1", "h2") else 1
            assert x == 0 or a > max(self.mlp_at)
            assert not any(y in self.tr_at for y in range(a + 1, a + nsteps))
            for y in range(nsteps):
                self.mlp_at[a + y] = (x, self.mlp_count[x] * y // nsteps, self.mlp_count[x] * (y + 1) // nsteps)
        assert max(self.mlp_at) < ns
        groups = [(s, dt) for s, v in self.tr_at.items() for _, dt in v]
        assert all(dt in (0, 1) for _, dt in groups)
        ahead = sum(dt for _, dt in groups)
        self.groups_by = [ahead + sum(s <= x for s, _ in groups) for x in range(ns)]
        self.mlp_before = [len({v[0] for s, v in self.mlp_at.items() if s < x}) for x in range(ns)]
        dve = [(1 if r.kind == "P" else 2) * (r.n * E + 64) for r in steps]
        pe = [r.n * E * 0.4 for r in steps]
        for s_, v in self.tr_at.items():
            pe[s_] += len(v) * GF // 2 * self.PASS
        for s_, (x, lo, hi) in self.mlp_at.items():
            pe[s_] += (hi - lo) * self.PASS * (1 if MLP[x][0] == "zt" else 2)
        self.sum_at, self.sum_end = {}, {}
        for k in range(self.nblk):
            a = self.blk_last[k] + 2
            b = (self.blk_last[k + 1] if k + 1 < self.nblk else ns + self.blk_last[0]) + 1
            lo, hi = 0.0, 9.0
            for _ in range(40):
                mid = (lo + hi) / 2
                w = [max(0.0, mid * dve[x % ns] * (1 + self.SUM_TILT[k] * (x - a) / (b - a)) - pe[x % ns])
                     for x in range(a, b)]
                lo, hi = (mid, hi) if sum(w) < E * self.PASS else (lo, mid)
            done = 0
            for x in range(a, b):
                end = E if x == b - 1 else round(E * sum(w[:x - a + 1]) / sum(w))
                if end > done:
                    self.put(self.sum_at, x, (k, done, end))
                    if end == E:
                        self.sum_end[k] = x
                done = end
        assert self.sum_end[self.nblk - 1] - ns < self.MLP_AT[1]
        assert self.MLP_AT[0] > (steps[ns - 1].kind == "D")

        self.load_first, self.load_last = {}, []
        for k in range(NG):
            uses = [s for s, r in enumerate(steps) if any(j // GF == k for _, j in r.pairs())]
            self.load_first.setdefault(min(uses), []).append(k)
            split = [x + 1 - dt * ns for x, v in self.lo_at.items() for (q, g), dt in v if g == k]
            self.load_last.append(max(uses + split))
        assert max(self.load_last) < ns

        self.w_need = [-(-max(r.w * E + a + cols for _, a, cols in r.runs()) // WCOLS) for r in steps]
        assert max(self.w_need) == WCH
        self.w_before, self.w_during = {}, {}
        lo_steps = sorted(s for s, v in self.lo_at.items() for _, dt in v if dt)
        for c in range(WCH):
            use = min(s for s in range(ns) if self.w_need[s] > c)
            s_ = min(use - self.W_LEAD, (c - self.W_AHEAD) * self.W_SPAN // (WCH - self.W_AHEAD))
            if c >= self.W_AHEAD:
                assert s_ >= 0
                self.w_during.setdefault(s_, []).append(c)
            else:
                self.w_before.setdefault(0 if c < self.W_FIRST else lo_steps[0] + 1, []).append(c)

    def put(self, table, s, what):
        dt = -(s // self.ns)
        table.setdefault(s % self.ns, []).append((what, dt))


def build_tower(nc, args, out):
    plan = Plan()
    steps, ns, nd, nblk = plan.steps, plan.ns, plan.nd, plan.nblk
    kc, kz = plan.kc, plan.kz
    ndmax = max(r.n for r in steps if r.kind == "D")
    tables = [args[f"tbl_{f}"] for f in range(NF)]
    ids, dense = args["ids"], args["dense_ctx"]
    out_rows = out.rearrange("(t b) o -> t (o b)", b=P)

    with ExitStack() as ctx:
        def sb(name, shape, dt=F32):
            return ctx.enter_context(nc.sbuf_tensor(name, shape, dt))

        def psum(name, shape, dt=F32):
            return ctx.enter_context(nc.psum_tensor(name, shape, dt))

        def sem(name):
            return ctx.enter_context(nc.semaphore(name))

        w_stack = sb("w_stack", [P, NPAIR * E], F32R)
        x_stack = sb("x_stack", [P, (NF + GF) * P], F32R)
        prod_blk = [sb(f"prod_blk{k}", [P, E, P]) for k in range(2)]
        prod_d = sb("prod_d", [P, DRING, ndmax * E])
        emb = [sb(f"emb{k}", [P, NF * E]) for k in range(2)]
        split = sb("split", [P, SRING, GF, 2, E])
        idx = [sb(f"idx{k}", [P, NF], I32) for k in range(2)]
        z = [sb(f"z{k}", [P, plan.nz + DENSE]) for k in range(2)]
        zt = [sb(f"zt{k}", [P, kc, P]) for k in range(2)]
        h1t = sb("h1t", [P, M1, P])
        h2t = sb("h2t", [P, M2, P])
        y_row = sb("y_row", [1, P])
        w1 = sb("w1", [P, kc, H1])
        w2 = sb("w2", [P, M1, H2])
        w3 = sb("w3", [P, M2])
        b1 = sb("b1", [P, M1])
        b2 = sb("b2", [P, M2])
        ident = sb("ident", [P, P])

        t_ps = psum("t_ps", [P, TRING, 2 * BANK])
        side_ps = psum("side_ps", [P, BANK])
        sum_ps = psum("sum_ps", [P, BANK])[:, 0:P]

        w_staged = [sem(f"w_staged{k}") for k in range(WBUF)]
        w_rounded = sem("w_rounded")
        w_split = sem("w_split")
        ident_in = sem("ident_in")
        consts_in = sem("consts_in")
        idx_in = [sem(f"idx_in{k}") for k in range(2)]
        dense_in = [sem(f"dense_in{k}") for k in range(2)]
        gathered = [[sem(f"gathered{k}_{g}") for g in range(NG)] for k in range(2)]
        gather_may_start = sem("gather_may_start")
        hi_done = sem("hi_done")
        lo_done = sem("lo_done")
        stack_tr = sem("stack_tr")
        stack_ready = sem("stack_ready")
        t_ready = sem("t_ready")
        prod_done = sem("prod_done")
        dsum_done = sem("dsum_done")
        bsum_done = sem("bsum_done")
        bsum_saved = sem("bsum_saved")
        mlp_done = sem("mlp_done")
        mlp_saved = sem("mlp_saved")
        y_stored = sem("y_stored")

        assert WBUF * WCOLS <= kc * H1 and WCH * WCOLS == NPAIR * E
        stage = [w1[:].rearrange("p k n -> p (k n)")[:, k * WCOLS:(k + 1) * WCOLS] for k in range(WBUF)]

        def group(buf, g):
            return emb[buf][:, g * GF * E:(g + 1) * GF * E].rearrange("p (f e) -> p f e", e=E)

        def t_slot(par, s):
            return ((par % 2) * ns + s) % TRING

        def pairs_of(r, buf, slot):
            if r.tail:
                xj = emb[buf][:, :].rearrange("p (b two e) -> p b two e", two=2, e=E)[:, :, 0, :]
                return t_ps[:, slot, 0:r.n * E].rearrange("p (n e) -> p n e", e=E), xj
            w = emb[buf][:, r.j0 * E:(r.j0 + r.nj) * E]
            xj = bass.AP(w.tensor, w.offset, [list(w.ap[0]), [E, 2], [E, r.nj], [1, E]])
            t = t_ps[:, slot, :].rearrange("p (two n e) -> p two n e", two=2, e=E)
            return t[:, :, 0:r.nj, :], xj

        def x_col(i, par):
            return (i + (GF if i >= NF - GF and par % 2 else 0)) * P

        def q_slot(par, q):
            return ((par % 2) * NG + q) % SRING

        assert 2 * ns % TRING == 0 and 2 * NG % SRING == 0 and 2 * nd % DRING == 0 and 2 * nblk % 2 == 0

        def w_chunks(s, prev, this, nxt):
            if prev or not nxt:
                return []
            return (plan.w_during if this else plan.w_before).get(s, [])

        def walk(engine, step, finish=None):
            last = TILES // 2 - 1
            for s in range(ns):
                step(s, -1, 1, False, False, True)
            for par in range(2):
                for s in range(ns):
                    step(s, 0, par, par > 0, True, True)
            with engine.Fori(1, last) as n:
                for par in range(2):
                    for s in range(ns):
                        step(s, n, par, True, True, True)
            for par in range(2):
                for s in range(ns):
                    step(s, last, par, True, True, par == 0)
            if finish:
                finish()
                return
            for s in range(ns):
                step(s, last + 1, 0, True, False, False)

        end = TILES - 1
        free = [((TILES - 1) * ns + s) % TRING for s in range(ns - TRING, ns)]
        h1_end = [side_ps[:, 0:BANK], t_ps[:, free[0], 0:BANK]]
        zt_end = t_ps[:, free[0], BANK:2 * BANK]
        h2_end = t_ps[:, free[1], 0:BANK]
        y_end = t_ps[:, free[1], BANK:2 * BANK]
        ZT_END, H1_END, H2_END, Y_END = end * NMLP + 1, end * NMLP + 2, end * NMLP + 4, end * NMLP + 5

        block = ctx.enter_context(nc.Block())

        @block.sync
        def _(sp):
            def load_rows(n, par):
                t = 2 * n + par
                for g in range(NG):
                    if not (isinstance(n, int) and n == 0):
                        sp.wait_ge(gathered[par][g], n * (GF * 16))
                sp.dma_start(idx[par][:, :], ids[bass.ds(t * P, P), :]).then_inc(idx_in[par], 16)
                if not (isinstance(n, int) and n == 0):
                    sp.wait_ge(mlp_done, n * (2 * NMLP) + ((par - 2) * NMLP + 1))
                sp.dma_start(z[par][:, plan.nz:plan.nz + DENSE], dense[bass.ds(t * P, P), :]).then_inc(dense_in[par], 16)

            load_rows(0, 0)
            load_rows(0, 1)
            w_bil = args["w_bil"]
            for c in range(WCH):
                if c >= WBUF:
                    sp.wait_ge(w_split, c - WBUF + 1)
                cols = w_bil[:, c * WCOLS:(c + 1) * WCOLS]
                four = bass.AP(cols.tensor, cols.offset, [[0, P // E]] + [list(x) for x in cols.ap])
                sp.dma_start(stage[c % WBUF], four).then_inc(w_staged[c % WBUF], 16)
            sp.wait_ge(w_split, WCH)
            for c, (a, m) in enumerate(plan.kchunks):
                sp.dma_start(w1[0:m, c, :], args["w1"][a:a + m, :]).then_inc(consts_in, 16)
            sp.dma_start(w2[:, :, :], args["W_top2"].rearrange("(k p) n -> p k n", p=P)).then_inc(consts_in, 16)
            sp.dma_start(w3[:, :], args["w3"]).then_inc(consts_in, 16)
            sp.dma_start(b1[:, :], args["b1"]).then_inc(consts_in, 16)
            sp.dma_start(b2[:, :], args["b2"]).then_inc(consts_in, 16)
            with sp.Fori(1, TILES // 2) as n:
                load_rows(n, 0)
                load_rows(n, 1)

        @block.gpsimd
        def _(pool):
            def gather(n, par, first):
                pool.wait_ge(idx_in[par], n * 16 + 16)
                pool.sem_inc(gather_may_start, 1)
                for g in plan.order:
                    if not first:
                        pool.wait_ge(prod_done, n * (2 * ns) + ((par - 2) * ns + plan.load_last[g] + 1))
                        pool.sem_inc(gather_may_start, 1)
                    for f in range(GF * g, GF * g + GF):
                        pool.indirect_dma_start(
                            out=emb[par][:, f * E:(f + 1) * E], out_offset=None, in_=tables[f],
                            in_offset=bass.IndirectOffsetOnAxis(ap=idx[par][:, f:f + 1], axis=0),
                        ).then_inc(gathered[par][g], 16)

            gather(0, 0, True)
            gather(0, 1, True)
            with pool.Fori(1, TILES // 2) as n:
                gather(n, 0, False)
                gather(n, 1, False)

        @block.scalar
        def _(act):
            act.dma_start(ident[:, :], args["ident"]).then_inc(ident_in, 16)

            def step(s, n, par, prev, this, nxt):
                live = {-1: prev, 0: this, 1: nxt}
                for c in w_chunks(s, prev, this, nxt):
                    act.wait_ge(w_staged[c % WBUF], 16 * (c // WBUF + 1))
                    act.copy(w_stack[:, c * WCOLS:(c + 1) * WCOLS], stage[c % WBUF]).then_inc(w_rounded, 1)
                for (q, g), dt in plan.hi_at.get(s, []):
                    if not live[dt]:
                        continue
                    buf, turn = (par + dt) % 2, (par + dt) // 2
                    act.wait_ge(gathered[buf][g], n * (GF * 16) + (turn + 1) * (GF * 16))
                    k = (2 * n + par + dt) * NG + q
                    if not (isinstance(k, int) and k < SRING):
                        act.wait_ge(stack_tr, k - SRING + 1)
                    act.copy(split[:, q_slot(par + dt, q), :, 0, :].bitcast(F32R),
                             group(buf, g)).then_inc(hi_done, 1)
                for (q, g), dt in plan.tr_at.get(s, []):
                    if not live[dt]:
                        continue
                    act.wait_ge(stack_tr, (2 * n + par + dt) * NG + (q + 1))
                    a = x_col(g * GF, par + dt)
                    stacks = x_stack[:, a:a + GF * P].rearrange("k (f two b) -> k f two b", two=2, b=P)
                    for odd in range(2):
                        for half in range(2):
                            act.copy(stacks[64 * half:64 * half + 64, :, odd, :],
                                     side_ps[64 * odd:64 * odd + 64, 0:GF // 2 * P].rearrange("k (f b) -> k f b", b=P)
                                     ).then_inc(stack_ready, 1)
                for (k, lo, hi), dt in plan.sum_at.get(s, []):
                    if hi < E or not live[dt]:
                        continue
                    act.wait_ge(bsum_done, (2 * n + par + dt) * nblk + (k + 1))
                    act.copy(zt[(par + dt) % 2][0:plan.blk_n[k], k, :], sum_ps[0:plan.blk_n[k], :]).then_inc(bsum_saved, 1)
                x, _, hi = plan.mlp_at.get(s, (0, 0, 0))
                if prev and hi and hi == plan.mlp_count[x]:
                    t = 2 * n + (par - 1)
                    what, m = MLP[x]
                    act.wait_ge(mlp_done, t * NMLP + (x + 1))
                    if what == "zt":
                        for c in range(nblk, kc):
                            rows = plan.kchunks[c][1]
                            i = act.copy(zt[(par - 1) % 2][0:rows, c, :],
                                         side_ps[0:rows, (c - nblk) * P:(c - nblk + 1) * P])
                    elif what == "h1":
                        i = act.activation(h1t[:, m, :], side_ps[:, 0:P], ACT.Relu, bias=b1[:, m:m + 1])
                    elif what == "h2":
                        for m in range(M2):
                            i = act.activation(h2t[:, m, :], side_ps[:, m * P:(m + 1) * P], ACT.Relu,
                                               bias=b2[:, m:m + 1])
                    else:
                        if not (isinstance(t, int) and t == 0):
                            act.wait_ge(y_stored, t * 16)
                        i = act.copy(y_row[:, :], side_ps[0:1, 0:P])
                    i.then_inc(mlp_saved, 1)
                    if what == "y":
                        act.wait_ge(mlp_saved, t * NMLP + NMLP)
                        act.dma_start(out_rows[bass.ds(t, 1), :], y_row[:, :]).then_inc(y_stored, 16)

            def finish():
                q = end % 2
                act.wait_ge(mlp_done, ZT_END)
                for c in range(nblk, kc):
                    rows = plan.kchunks[c][1]
                    i = act.copy(zt[q][0:rows, c, :], zt_end[0:rows, (c - nblk) * P:(c - nblk + 1) * P])
                i.then_inc(mlp_saved, 1)
                act.wait_ge(bsum_done, TILES * nblk)
                act.copy(zt[q][0:plan.blk_n[nblk - 1], nblk - 1, :],
                         sum_ps[0:plan.blk_n[nblk - 1], :]).then_inc(bsum_saved, 1)
                for x in range(2):
                    act.wait_ge(mlp_done, H1_END + x)
                    for m in range(x * M1 // 2, (x + 1) * M1 // 2):
                        i = act.activation(h1t[:, m, :], h1_end[x][:, m % 2 * P:(m % 2 + 1) * P], ACT.Relu,
                                           bias=b1[:, m:m + 1])
                    i.then_inc(mlp_saved, 1)
                act.wait_ge(mlp_done, H2_END)
                for m in range(M2):
                    i = act.activation(h2t[:, m, :], h2_end[:, m * P:(m + 1) * P], ACT.Relu, bias=b2[:, m:m + 1])
                i.then_inc(mlp_saved, 1)
                act.wait_ge(mlp_done, Y_END)
                act.wait_ge(y_stored, end * 16)
                act.copy(y_row[:, :], y_end[0:1, 0:P]).then_inc(mlp_saved, 1)
                act.wait_ge(mlp_saved, Y_END)
                act.dma_start(out_rows[end:end + 1, :], y_row[:, :]).then_inc(y_stored, 16)

            walk(act, step, finish)
            act.wait_ge(y_stored, 16 * TILES)

        @block.vector
        def _(dve):
            def step(s, n, par, prev, this, nxt):
                live = {-1: prev, 0: this, 1: nxt}
                t = 2 * n + par
                for c in w_chunks(s, prev, this, nxt):
                    dve.wait_ge(w_staged[c % WBUF], 16 * (c // WBUF + 1))
                    dve.wait_ge(w_rounded, c + 1)
                    cols = w_stack[64:128, c * WCOLS:(c + 1) * WCOLS]
                    dve.tensor_tensor(cols, stage[c % WBUF][64:128, :], cols.bitcast(F32), ALU.subtract).then_inc(w_split, 1)
                r = steps[s]
                if this:
                    for g in plan.load_first.get(s, []):
                        dve.wait_ge(gathered[par][g], n * (GF * 16) + GF * 16)
                    dve.wait_ge(t_ready, t * ns + (s + 1))
                    tv, xj = pairs_of(r, par, t_slot(par, s))
                    if r.kind == "P":
                        k = r.block
                        done = t * nblk + (k - 1)
                        if s == plan.blk_first[k] and not (isinstance(done, int) and done <= 0):
                            dve.wait_ge(bsum_done, done)
                        dst = prod_blk[(par * nblk + k) % 2][:, :, r.off:r.off + r.n].rearrange(
                            "p e (two n) -> p two n e", two=2)
                        dve.tensor_tensor(dst, tv, xj, ALU.mult).then_inc(prod_done, 1)
                    else:
                        k = plan.d_index[s]
                        done = t * nd + (k - DRING + 1)
                        if not (isinstance(done, int) and done <= 0):
                            dve.wait_ge(dsum_done, done)
                        dst = prod_d[:, (par * nd + k) % DRING, 0:r.n * E]
                        if r.tail:
                            dst = dst.rearrange("p (n e) -> p n e", e=E)
                        else:
                            dst = dst.rearrange("p (two n e) -> p two n e", two=2, e=E)
                        dve.tensor_tensor(dst, tv, xj, ALU.mult).then_inc(prod_done, 1)
                b, dt = (s - 1, 0) if s else (ns - 1, -1)
                if live[dt] and steps[b].kind == "D":
                    rb, k = steps[b], plan.d_index[b]
                    if k == 0 and not (isinstance(n, int) and t < 2):
                        dve.wait_ge(mlp_done, (t - 2) * NMLP + 1)
                    dve.wait_ge(prod_done, (t + dt) * ns + (b + 1))
                    dve.tensor_reduce(z[(par + dt) % 2][:, rb.z - plan.zd:rb.z - plan.zd + rb.n],
                                      prod_d[:, ((par + dt) * nd + k) % DRING, 0:rb.n * E].rearrange("p (n e) -> p n e", e=E),
                                      AX.X, ALU.add).then_inc(dsum_done, 1)
                for (q, g), dt in plan.lo_at.get(s, []):
                    if not live[dt]:
                        continue
                    buf = (par + dt) % 2
                    dve.wait_ge(hi_done, (t + dt) * NG + (q + 1))
                    part = split[:, q_slot(par + dt, q), :, :, :]
                    dve.tensor_tensor(part[:, :, 1, :], group(buf, g), part[:, :, 0, :],
                                      ALU.subtract).then_inc(lo_done, 1)

            walk(dve, step)

        @block.tensor
        def _(pe):
            pe.wait_ge(ident_in, 16)

            def sum_block(t, q, k, lo, hi):
                if lo == 0:
                    pe.wait_ge(prod_done, t * ns + (plan.blk_last[k] + 1))
                    done = t * nblk + k
                    if not (isinstance(done, int) and done <= 0):
                        pe.wait_ge(bsum_saved, done)
                for e in range(lo, hi):
                    m = pe.matmul(sum_ps[0:plan.blk_n[k], :], prod_blk[(q * nblk + k) % 2][:, e, 0:plan.blk_n[k]],
                                  ident[:, :], start=(e == 0), stop=(e == E - 1), is_transpose=True)
                if hi == E:
                    m.then_inc(bsum_done, 1)

            def step(s, n, par, prev, this, nxt):
                live = {-1: prev, 0: this, 1: nxt}
                t = 2 * n + par
                for (q, g), dt in plan.tr_at.get(s, []):
                    if not live[dt]:
                        continue
                    k = (t + dt) * NG + q
                    pe.wait_ge(lo_done, k + 1)
                    if not (isinstance(k, int) and k == 0):
                        pe.wait_ge(stack_ready, k * 4)
                    begun = (t - 1) * NMLP + plan.mlp_before[s]
                    if prev and not (isinstance(begun, int) and begun <= 0):
                        pe.wait_ge(mlp_saved, begun)
                    for f in range(GF // 2):
                        a = split[:, q_slot(par + dt, q), 2 * f:2 * f + 2, :, :].rearrange("p f h e -> p (f h e)")
                        m = pe.transpose(side_ps[:, f * P:(f + 1) * P], a, ident[:, :])
                    m.then_inc(stack_tr, 1)
                if this:
                    r = steps[s]
                    if isinstance(n, int) and t == 0:
                        pe.wait_ge(w_split, plan.w_need[s])
                    q = max(plan.order.index(i // GF) for i in r.ii)
                    pe.wait_ge(stack_ready, t * (4 * NG) + (q + 1) * 4)
                    if not (isinstance(n, int) and t * ns + s < TRING):
                        pe.wait_ge(prod_done, t * ns + (s - TRING + 1))
                    for x, (i, a, cols) in enumerate(r.runs()):
                        m = pe.matmul(t_ps[:, t_slot(par, s), x * BANK:x * BANK + cols],
                                      x_stack[:, x_col(i, par):x_col(i, par) + P],
                                      w_stack[:, r.w * E + a:r.w * E + a + cols], start=True, stop=True)
                    m.then_inc(t_ready, 1)
                for (k, lo, hi), dt in plan.sum_at.get(s, []):
                    if live[dt]:
                        sum_block(t + dt, (par + dt) % 2, k, lo, hi)
                if prev and s in plan.mlp_at:
                    x, lo, hi = plan.mlp_at[s]
                    what, j = MLP[x]
                    u = 2 * n + (par - 1)
                    q = (par - 1) % 2
                    if lo == 0:
                        before = u * NMLP + x
                        if not (isinstance(before, int) and before == 0):
                            pe.wait_ge(mlp_saved, before)
                        groups = t * NG + plan.groups_by[s]
                        if isinstance(groups, int):
                            groups = min(groups, TILES * NG)
                        pe.wait_ge(stack_ready, groups * 4)
                        if what == "zt":
                            pe.wait_ge(dsum_done, u * nd + nd)
                            pe.wait_ge(dense_in[q], n * 16 + ((par - 1) // 2) * 16 + 16)
                        if (what, j) == ("h1", 0):
                            if isinstance(u, int) and u == 0:
                                pe.wait_ge(consts_in, 16 * (kc + 4))
                            pe.wait_ge(bsum_saved, u * nblk + nblk)
                    for c in range(lo, hi):
                        if what == "zt":
                            w = plan.kchunks[nblk + c][1]
                            i = pe.transpose(side_ps[0:w, c * P:(c + 1) * P], z[q][:, c * P:c * P + w], ident[:, :])
                        elif what == "h1":
                            w = plan.kchunks[c][1]
                            i = pe.matmul(side_ps[:, 0:P], w1[0:w, c, j * P:(j + 1) * P],
                                          zt[q][0:w, c, :], start=(c == 0), stop=(c == kc - 1))
                        elif what == "h2":
                            m, k = divmod(c, M1)
                            i = pe.matmul(side_ps[:, m * P:(m + 1) * P], w2[:, k, m * P:(m + 1) * P],
                                          h1t[:, k, :], start=(k == 0), stop=(k == M1 - 1))
                        else:
                            i = pe.matmul(side_ps[0:1, 0:P], w3[:, c:c + 1], h2t[:, c, :],
                                          start=(c == 0), stop=(c == M2 - 1))
                    if hi == plan.mlp_count[x]:
                        i.then_inc(mlp_done, 1)

            def finish():
                q = end % 2

                def layer1(x, c):
                    w, first, last = plan.kchunks[c][1], x * M1 // 2, (x + 1) * M1 // 2
                    for m in range(first, last):
                        i = pe.matmul(h1_end[x][:, m % 2 * P:(m % 2 + 1) * P], w1[0:w, c, m * P:(m + 1) * P],
                                      zt[q][0:w, c, :], start=(c == 0 and m == first), stop=(c == nblk - 1 and m == last - 1))
                    return i

                pe.wait_ge(mlp_saved, end * NMLP)
                for c in range(nblk - 1):
                    pe.wait_ge(bsum_saved, end * nblk + c + 1)
                    layer1(0, c)
                pe.wait_ge(prod_done, TILES * ns - TRING + 1)
                for c in range(nblk - 1):
                    layer1(1, c)
                pe.wait_ge(dsum_done, TILES * nd)
                pe.wait_ge(dense_in[q], TILES // 2 * 16)
                for c in range(kz):
                    w = plan.kchunks[nblk + c][1]
                    i = pe.transpose(zt_end[0:w, c * P:(c + 1) * P], z[q][:, c * P:c * P + w], ident[:, :])
                i.then_inc(mlp_done, 1)
                for s in range(ns):
                    for (k, lo, hi), dt in plan.sum_at.get(s, []):
                        if dt == -1:
                            sum_block(end, q, k, lo, hi)
                pe.wait_ge(mlp_saved, ZT_END)
                for x in range(2):
                    for c in range(nblk, kc):
                        layer1(x, c)
                    if x == 0:
                        pe.wait_ge(bsum_saved, TILES * nblk)
                    layer1(x, nblk - 1).then_inc(mlp_done, 1)
                for k in range(M1):
                    if k % (M1 // 2) == 0:
                        pe.wait_ge(mlp_saved, H1_END + k // (M1 // 2))
                    for m in range(M2):
                        i = pe.matmul(h2_end[:, m * P:(m + 1) * P], w2[:, k, m * P:(m + 1) * P], h1t[:, k, :],
                                      start=(k == 0 and m == 0), stop=(k == M1 - 1 and m == M2 - 1))
                i.then_inc(mlp_done, 1)
                pe.wait_ge(mlp_saved, H2_END)
                for c in range(M2):
                    i = pe.matmul(y_end[0:1, 0:P], w3[:, c:c + 1], h2t[:, c, :], start=(c == 0), stop=(c == M2 - 1))
                i.then_inc(mlp_done, 1)

            walk(pe, step, finish)


def kernel(**inputs):
    from concourse import bacc
    from concourse.bass_utils import run_bass_kernel_spmd

    plan = Plan()
    def numbers(pairs):
        return [min(p) * (2 * NF - min(p) - 1) // 2 + (max(p) - min(p) - 1) for p in pairs]

    w_top1 = np.asarray(inputs["W_top1"])
    w_bil = np.asarray(inputs["L0_rec_bilinear_matrices"])[numbers(plan.w_pairs)]
    swapped = np.array([i > j for i, j in plan.w_pairs])
    w_bil[swapped] = w_bil[swapped].transpose(0, 2, 1)
    host = {
        "dense_ctx": np.asarray(inputs["dense_ctx"]),
        "ids": np.asarray(inputs["ids"]),
        "w_bil": np.ascontiguousarray(w_bil.transpose(1, 0, 2).reshape(E, NPAIR * E)),
        "w1": np.ascontiguousarray(w_top1[numbers(plan.pairs) + list(range(NPAIR, DIN))]),
        "W_top2": np.asarray(inputs["W_top2"]),
        "w3": np.ascontiguousarray(np.asarray(inputs["W_top3"]).reshape(M2, P).T),
        "b1": np.ascontiguousarray(np.asarray(inputs["b_top1"]).reshape(M1, P).T),
        "b2": np.ascontiguousarray(np.asarray(inputs["b_top2"]).reshape(M2, P).T),
        "ident": np.eye(P, dtype=np.float32),
    }
    for f in range(NF):
        host[f"tbl_{f}"] = np.asarray(inputs[f"tbl_{f}"])

    nc = bacc.Bacc("TRN2", target_bir_lowering=False, num_devices=1)
    arrays, args = {}, {}
    for name, a in host.items():
        a = np.ascontiguousarray(a)
        arrays[f"in_{name}"] = a
        args[name] = nc.dram_tensor(f"in_{name}", a.shape, mybir.dt.from_np(a.dtype), kind="ExternalInput").ap()
    out = nc.dram_tensor("out_y", (B, 1), F32, kind="ExternalOutput").ap()
    build_tower(nc, args, out)
    r = run_bass_kernel_spmd(nc, [arrays], core_ids=[0])
    return r.results[0]["out_y"]
```
